# Optimizing a Trainium2 kernel written in Bass

```python
import numpy as np
import jax
import jax.numpy as jnp

def _softmax(x, axis=-1):
    return jax.nn.softmax(x, axis=axis)

def _gelu(x):
    return jax.nn.gelu(x, approximate=True)

def _silu(x):
    return jax.nn.silu(x)

def _sigmoid(x):
    return jax.nn.sigmoid(x)

def _layernorm(x, axis=-1, eps=1e-05):
    m = jnp.mean(x, axis=axis, keepdims=True)
    v = jnp.var(x, axis=axis, keepdims=True)
    return (x - m) / jnp.sqrt(v + eps)

def _scatter_add(tgt, idx, src, axis=0):
    return tgt.at[idx].add(src)

def _segment_sum(src, seg, n):
    return jax.ops.segment_sum(src, seg, n)
kernel_name = 'mk_seq_preln_d1_jaxref_r4_cc7249'

def setup_inputs(seed: int=0):
    np.random.seed(seed)
    _w = jnp.asarray

    def _L0_attn_setup():
        import jax, jax.numpy as jnp
        import numpy as np
        NEG = -1000000000.0

        def _attention(x, Wq, bq, Wk, bk, Wv, bv, Wo, num_heads=16):
            B, N, E = x.shape
            H = num_heads
            D = E // H
            scale = D ** (-0.5)
            q = (jnp.einsum('bne,fe->bnf', x, Wq) + bq).reshape(B, N, H, D).transpose(0, 2, 1, 3)
            k = (jnp.einsum('bne,fe->bnf', x, Wk) + bk).reshape(B, N, H, D).transpose(0, 2, 1, 3)
            v = (jnp.einsum('bne,fe->bnf', x, Wv) + bv).reshape(B, N, H, D).transpose(0, 2, 1, 3)
            scores = jnp.einsum('bhqd,bhkd->bhqk', q, k) * scale
            scores = scores.at[:, :, 0, -1].set(NEG)
            scores = scores.at[:, :, -1, 0].set(NEG)
            weights = jax.nn.softmax(scores, axis=-1)
            out = jnp.einsum('bhqk,bhkd->bhqd', weights, v)
            out = out.transpose(0, 2, 1, 3).reshape(B, N, E)
            return jnp.einsum('bne,fe->bnf', out, Wo)
        key = jax.random.key(seed)
        ks = jax.random.split(key, 8)
        B, N, E = (4, 512, 256)
        s = E ** (-0.5)
        return {'x': jax.random.normal(ks[0], (B, N, E), jnp.float32), 'Wq': jax.random.normal(ks[1], (E, E), jnp.float32) * s, 'bq': jax.random.normal(ks[2], (E,), jnp.float32) * 0.02, 'Wk': jax.random.normal(ks[3], (E, E), jnp.float32) * s, 'bk': jax.random.normal(ks[4], (E,), jnp.float32) * 0.02, 'Wv': jax.random.normal(ks[5], (E, E), jnp.float32) * s, 'bv': jax.random.normal(ks[6], (E,), jnp.float32) * 0.02, 'Wo': jax.random.normal(ks[7], (E, E), jnp.float32) * s}
    _L0_attn_in = _L0_attn_setup()

    def _L0_ffn_setup():
        import jax, jax.numpy as jnp
        import numpy as np
        B, T, D, E, FF, K = (4, 256, 256, 8, 512, 2)
        SINKHORN_ITERS = 3

        def _sinkhorn(log_alpha, iters=SINKHORN_ITERS):
            for _ in range(iters):
                log_alpha = log_alpha - jax.nn.logsumexp(log_alpha, axis=-1, keepdims=True)
                log_alpha = log_alpha - jax.nn.logsumexp(log_alpha, axis=-2, keepdims=True)
            gates = jnp.exp(log_alpha)
            return gates / (jnp.sum(gates, axis=-1, keepdims=True) + 1e-08)
        key = jax.random.key(seed)
        ks = jax.random.split(key, 7)
        scale = 0.02
        return {'x': jax.random.normal(ks[0], (B, T, D), dtype=jnp.float32), 'router_w': jax.random.normal(ks[1], (E, D), dtype=jnp.float32) * scale, 'router_b': jnp.zeros((E,), dtype=jnp.float32), 'temperature': jnp.ones((1,), dtype=jnp.float32) * 0.5, 'wg': jax.random.normal(ks[2], (E, D, FF), dtype=jnp.float32) * scale, 'wp': jax.random.normal(ks[3], (E, D, FF), dtype=jnp.float32) * scale, 'wo': jax.random.normal(ks[4], (E, FF, D), dtype=jnp.float32) * scale}
    _L0_ffn_in = _L0_ffn_setup()
    _d = {'L0_attn_x': _L0_attn_in['x'], 'L0_attn_Wq': _L0_attn_in['Wq'], 'L0_attn_bq': _L0_attn_in['bq'], 'L0_attn_Wk': _L0_attn_in['Wk'], 'L0_attn_bk': _L0_attn_in['bk'], 'L0_attn_Wv': _L0_attn_in['Wv'], 'L0_attn_bv': _L0_attn_in['bv'], 'L0_attn_Wo': _L0_attn_in['Wo'], 'L0_ffn_router_w': _L0_ffn_in['router_w'], 'L0_ffn_router_b': _L0_ffn_in['router_b'], 'L0_ffn_temperature': _L0_ffn_in['temperature'], 'L0_ffn_wg': _L0_ffn_in['wg'], 'L0_ffn_wp': _L0_ffn_in['wp'], 'L0_ffn_wo': _L0_ffn_in['wo']}
    _x0 = _d['L0_attn_x']
    _d['L0_attn_x'] = jax.random.normal(jax.random.fold_in(jax.random.key(seed), 1), (16, 512, 256), dtype=_x0.dtype)
    del _x0
    return _d

def reference(L0_attn_x, L0_attn_Wq, L0_attn_bq, L0_attn_Wk, L0_attn_bk, L0_attn_Wv, L0_attn_bv, L0_attn_Wo, L0_ffn_router_w, L0_ffn_router_b, L0_ffn_temperature, L0_ffn_wg, L0_ffn_wp, L0_ffn_wo):

    def _L0_attn_ref(x, Wq, bq, Wk, bk, Wv, bv, Wo):
        import jax, jax.numpy as jnp
        import numpy as np
        NEG = -1000000000.0

        def _attention(x, Wq, bq, Wk, bk, Wv, bv, Wo, num_heads=16):
            B, N, E = x.shape
            H = num_heads
            D = E // H
            scale = D ** (-0.5)
            q = (jnp.einsum('bne,fe->bnf', x, Wq) + bq).reshape(B, N, H, D).transpose(0, 2, 1, 3)
            k = (jnp.einsum('bne,fe->bnf', x, Wk) + bk).reshape(B, N, H, D).transpose(0, 2, 1, 3)
            v = (jnp.einsum('bne,fe->bnf', x, Wv) + bv).reshape(B, N, H, D).transpose(0, 2, 1, 3)
            scores = jnp.einsum('bhqd,bhkd->bhqk', q, k) * scale
            scores = scores.at[:, :, 0, -1].set(NEG)
            scores = scores.at[:, :, -1, 0].set(NEG)
            weights = jax.nn.softmax(scores, axis=-1)
            out = jnp.einsum('bhqk,bhkd->bhqd', weights, v)
            out = out.transpose(0, 2, 1, 3).reshape(B, N, E)
            return jnp.einsum('bne,fe->bnf', out, Wo)
        return _attention(x, Wq, bq, Wk, bk, Wv, bv, Wo, num_heads=16)

    def _L0_ffn_ref(x, router_w, router_b, temperature, wg, wp, wo):
        import jax, jax.numpy as jnp
        import numpy as np
        B, T, D, E, FF, K = (4, 256, 256, 8, 512, 2)
        SINKHORN_ITERS = 3

        def _sinkhorn(log_alpha, iters=SINKHORN_ITERS):
            for _ in range(iters):
                log_alpha = log_alpha - jax.nn.logsumexp(log_alpha, axis=-1, keepdims=True)
                log_alpha = log_alpha - jax.nn.logsumexp(log_alpha, axis=-2, keepdims=True)
            gates = jnp.exp(log_alpha)
            return gates / (jnp.sum(gates, axis=-1, keepdims=True) + 1e-08)
        temp = jnp.maximum(temperature, 0.1)
        scores = (jnp.einsum('btd,ed->bte', x, router_w) + router_b) / temp
        gates = _sinkhorn(scores)
        topk_vals, topk_idx = jax.lax.top_k(gates, K)
        topk_gates = topk_vals / (jnp.sum(topk_vals, axis=-1, keepdims=True) + 1e-08)
        g = jax.nn.relu(jnp.einsum('btd,edf->btef', x, wg))
        p = jnp.einsum('btd,edf->btef', x, wp)
        all_out = jnp.einsum('btef,efd->bted', g * p, wo)
        gathered = jnp.take_along_axis(all_out, topk_idx[..., None], axis=2)
        expert_out = jnp.sum(gathered * topk_gates[..., None], axis=2)
        return x + expert_out
    x = L0_attn_x
    x = x + _L0_attn_ref(_layernorm(x, axis=-1), L0_attn_Wq, L0_attn_bq, L0_attn_Wk, L0_attn_bk, L0_attn_Wv, L0_attn_bv, L0_attn_Wo)
    x = x + _L0_ffn_ref(_layernorm(x, axis=-1), L0_ffn_router_w, L0_ffn_router_b, L0_ffn_temperature, L0_ffn_wg, L0_ffn_wp, L0_ffn_wo)
    return x

_drawn_inputs = setup_inputs


def setup_inputs(seed=0):
    import zlib

    import numpy as np

    out = dict(_drawn_inputs(seed))
    spreads = {'L0_ffn_router_b': (0.0, 0.8)}
    factors = {'L0_attn_bq': 8.0,
     'L0_attn_bk': 8.0,
     'L0_attn_bv': 2.841,
     'L0_ffn_router_w': 5.429,
     'L0_ffn_wg': 5.77,
     'L0_ffn_wp': 4.767,
     'L0_ffn_wo': 4.764}
    for name, (base, spread) in spreads.items():
        noise = np.random.default_rng([zlib.crc32(name.encode()), seed]).standard_normal(out[name].shape)
        drawn = base * np.exp(spread * noise) if base else spread * noise
        out[name] = jnp.asarray(drawn.astype(out[name].dtype))
    for name, factor in factors.items():
        out[name] = (out[name] * factor).astype(out[name].dtype)
    return out
```

```python
from contextlib import ExitStack

import concourse.bass as bass
from concourse import mybir

ALU = mybir.AluOpType
ACT = mybir.ActivationFunctionType
AX_X = mybir.AxisListType.X
F32 = mybir.dt.float32
U32 = mybir.dt.uint32
BF16 = mybir.dt.bfloat16

P = 128
NEG = -1.0e9
LN_EPS = 1e-5

Q_PART = (0, 0, 1, 0, 2, 1)
K_PART = (0, 1, 0, 2, 0, 1)
PAIRS = len(Q_PART)

MISC = [
    (0, 2, "max_rows", 3, "act", "prev"),
    (0, 4, "q_proj", 1, "act", "cur"),
    (0, 6, "k_proj", 1, "act", "cur"),
    (0, 9, "out_rows", 1, "dve", "prev"),
    (1, 2, "max_rows", 0, "act", "cur"),
    (1, 5, "v_proj", 0, "dve", "cur"),
    (1, 9, "out_rows", 2, "dve", "prev"),
    (2, 2, "max_rows", 1, "act", "cur"),
    (2, 4, "v_proj", 1, "dve", "cur"),
    (2, 5, "x_cols", 0, "act", "next"),
    (2, 7, "x_cols", 1, "act", "next"),
    (2, 9, "out_rows", 3, "dve", "prev"),
    (2, 10, "q_proj", 0, "act", "next"),
    (2, 11, "k_proj", 0, "act", "next"),
    (2, 12, "att_cols", 0, "act", "prev"),
    (2, 13, "att_cols", 1, "act", "prev"),
    (3, 0, "att_out", 0, "dve", "prev"),
    (3, 1, "att_out", 1, "dve", "prev"),
    (3, 2, "max_rows", 2, "act", "cur"),
    (3, 9, "out_rows", 0, "dve", "cur"),
    (3, 11, "xn_cols", 0, "act", "prev"),
    (3, 12, "xn_cols", 1, "act", "prev"),
    (3, 14, "router", 0, "dve", "prev"),
]


def same_batch(arg):
    return arg < 3


def present(b, who):
    return {"cur": b < 16, "prev": b > 0, "next": b < 15}[who]


def bank_of(name, arg):
    return [(n, a) for _, _, n, a, _, _ in MISC].index((name, arg)) % 2


def jobs_before(b, name, arg):
    n = 0
    for i, (_, _, other, a, _, who) in enumerate(MISC):
        if who == "next" and (other, a) == (name, arg) and not present(b, who):
            raise ValueError("no such job")
        if (other, a) == (name, arg):
            return n
        if i % 2 == bank_of(name, arg) and present(b, who):
            n += 1
    raise ValueError(name)


def jobs_in(b, bank):
    return sum(1 for i, j in enumerate(MISC) if i % 2 == bank and present(b, j[5]))


def filled(b, name, arg):
    bank = bank_of(name, arg)
    if isinstance(b, int):
        return sum(jobs_in(i, bank) for i in range(b)) + jobs_before(b, name, arg) + 1
    return b * jobs_in(1, bank) + (jobs_in(0, bank) - jobs_in(1, bank) + jobs_before(1, name, arg) + 1)


def build(nc, x, Wq, bq, Wk, bk, Wv, bv, Wo, router_w, router_b, temperature, wg, wp, wo, out, dbg=None):
    B, N, E = x.shape
    H, D = 16, E // 16
    NE, _, FF = wg.shape
    KT = E // P
    TT = N // P
    GROUPS, GH = 4, 4
    STEP = GH * TT
    UNITS = GROUPS * STEP
    QROWS = PAIRS * D
    MASK_ROW = QROWS
    MAX_ROW = QROWS + 2
    SROWS = MAX_ROW + 3
    K_LAST, K_FIRST, ONES, Q_FIRST, Q_LAST = range(5)
    BATCH_TILES = B * TT
    SCALE = float(D) ** -0.5
    J = BATCH_TILES
    TOP = 2
    REGION = B * N + P
    MIN_TILES = TOP * B * N // P
    NT = (TOP * B * N + NE * (P - 1)) // P
    ROW = E + 2
    FT = FF // P
    assert out.shape[0] == B * N + P
    assert (B, TT, KT, H) == (16, 4, 2, 16)

    with ExitStack() as ctx:
        def sb(name, shape, dt):
            return ctx.enter_context(nc.sbuf_tensor(name, shape, dt))

        def psum(name, shape, dt):
            return ctx.enter_context(nc.psum_tensor(name, shape, dt))

        def sem(name):
            return ctx.enter_context(nc.semaphore(name))

        s1 = psum("s1", [P, 2, 512], F32)
        s2 = psum("s2", [P, 3, 512], F32)
        pv = psum("pv", [P, 512], F32)
        misc = psum("misc", [P, 2, 512], F32)

        stacks = sb("stacks", [P, 2, H, N], BF16)
        qst = stacks[:, 0, :, :]
        kst = stacks[:, 1, :, :]
        ring = sb("ring", [P, 2 * TOP * TT * ROW], F32)
        prob = ring[:, 0:2 * GH * N].rearrange("p (a h n) -> p a h n", a=2, h=GH)
        vau = sb("vau", [P, TT, H, 2 * D], F32)
        xin = sb("xin", [P, TT, E], F32)
        xc = sb("xc", [P, KT, N], F32)
        qk32 = sb("qk32", [P, 2, 2, N], F32)
        rest = sb("rest", [P, N], F32)
        parts = sb("parts", [P, 2, 2, 3, N], BF16)
        o32 = sb("o32", [P, N], F32)
        att = sb("att", [P, TT, E], F32)
        attc = sb("attc", [P, KT, N], F32)
        xres = sb("xres", [P, TT, E], F32)
        xn = sb("xn", [P, TT, E], F32)
        xnc = sb("xnc", [P, KT, N], F32)
        rden = sb("rden", [P, TT, GH], F32)
        mx = sb("mx", [P, 2, TT, GH], F32)
        negm = sb("negm", [GH, N], F32)
        mrest = sb("mrest", [GH, N], F32)
        mparts = sb("mparts", [GH, 3, N], BF16)
        stats = sb("stats", [P, 2, TT, 6], F32)
        mv = sb("mv", [P, 2, TT, 2], F32)
        rstd = sb("rstd", [P, 2, TT], F32)
        varp = sb("varp", [P, 2, TT], F32)
        nhalf = sb("nhalf", [P, TT], F32)
        ident = sb("ident", [P, P], F32)
        wqT = sb("wqT", [P, KT, E], F32)
        wkT = sb("wkT", [P, KT, E], F32)
        wvT = sb("wvT", [P, KT, E], F32)
        woT = sb("woT", [P, KT, E], F32)
        wnat = prob[:, 0, 0:4, :].rearrange("p m (f e) -> p m f e", f=2)
        bias = sb("bias", [P, 2, 2], F32)
        bvb = sb("bvb", [P, E], F32)
        rw = sb("rw", [NE, E], F32)
        rwT = sb("rwT", [P, KT, NE], F32)
        rbb = sb("rbb", [P, NE], F32)
        tmp1 = sb("tmp1", [P, 1], F32)
        tinv = sb("tinv", [P, 1], F32)
        sc = sb("sc", [P, TT, B, NE], F32)
        edge = sb("edge", [1, 5, N], BF16)

        free = qk32[:, :, :, :].rearrange("p a b n -> p (a b n)")
        gates = free[:, 0:512].rearrange("p (j e) -> p j e", e=NE)
        work = free[:, 512:1024].rearrange("p (j e) -> p j e", e=NE)
        sel = free[:, 1024:2048].rearrange("p (c j e) -> p c j e", c=TOP, e=NE)
        colla = rest[:, :]
        rowm = sb("rowm", [P, J], F32)
        rowl = sb("rowl", [P, J], F32)
        colm = sb("colm", [P, 4], F32)
        topv = sb("topv", [P, TOP, J], F32)
        posf = sb("posf", [P, J], F32)
        posu = sb("posu", [P, TOP, J], U32)
        lower = sb("lower", [P, P], F32)
        ones = sb("ones", [P, P], F32)
        tokf = sb("tokf", [P, J], F32)
        rev = sb("rev", [P, NE], F32)
        regoff = sb("regoff", [P, NE], F32)
        pidx = sb("pidx", [P, 1], F32)
        kk = sb("kk", [1, J], F32)
        ti = sb("ti", [1, NT], F32)
        cmp1 = o32[0:1, :].rearrange("p (e j) -> p e j", e=NE)
        free1 = parts[0:1, :, :, :, :].rearrange("p a b c n -> p (a b c n)").bitcast(F32)
        cmp2 = free1[:, 0:NT * NE].rearrange("p (t e) -> p t e", e=NE)
        cmp3 = free1[:, NT * NE:2 * NT * NE].rearrange("p (t e) -> p t e", e=NE)
        tiles = sb("tiles", [1, 2, NE], F32)
        tabf = sb("tabf", [1, 3, NT], F32)
        tabu = sb("tabu", [1, 2, NT], U32)
        padf = sb("padf", [P, NE], F32)
        padu = sb("padu", [P, NE], U32)
        padrow = sb("padrow", [P, ROW], F32)
        srow = ring[:, :].rearrange("p (a c t r) -> p a c t r", a=2, c=TOP, t=TT)
        sidx = sb("sidx", [P, 2, TOP, TT], U32)
        wgs = sb("wgs", [P, NE * KT, FF], F32)
        wps = sb("wps", [P, NE * KT, FF], F32)
        wos = stacks[:, :, :, :].rearrange("p a h n -> p (a h n)").bitcast(F32).rearrange("p (f e) -> p f e", e=E)
        gsb, hsb = xc[:, 0, :], xc[:, 1, :]
        hT = attc[:, 0, :].rearrange("p (f n) -> p f n", f=FT)
        tinT = attc[:, 1, 0:KT * P].rearrange("p (k n) -> p k n", k=KT)
        tin, ysb = xnc[:, 0, 0:ROW], xnc[:, 1, 0:E]
        meta = sb("meta", [P, 2, 2], F32)
        yidx = sb("yidx", [P, 1], U32)

        xn_d = nc.dram_tensor("xn_scratch", (B * N, E), F32, kind="Internal").ap()
        slots_d = nc.dram_tensor("slots_scratch", (NE * REGION + (NT - MIN_TILES + 1) * P, ROW), F32, kind="Internal").ap()

        passed = sem("passed")
        w_loaded = sem("w_loaded")
        small_loaded = sem("small_loaded")
        const_set = sem("const_set")
        edge_set = sem("edge_set")
        edges_placed = sem("edges_placed")
        ident_set = sem("ident_set")
        w_turned = sem("w_turned")
        w_copied = sem("w_copied")
        bias_scaled = sem("bias_scaled")
        x_loaded = sem("x_loaded")
        xres_loaded = sem("xres_loaded")
        ln_stats = [sem("ln1_stats"), sem("ln2_stats")]
        ln_mean = [sem("ln1_mean"), sem("ln2_mean")]
        ln_varp = [sem("ln1_varp"), sem("ln2_varp")]
        ln_rstd = [sem("ln1_rstd"), sem("ln2_rstd")]
        ln_done = [sem("ln1_done"), sem("ln2_done")]
        s1_full, s1_read = sem("s1_full"), sem("s1_read")
        s2_full, exp_done = sem("s2_full"), sem("exp_done")
        pv_part = sem("pv_part")
        o_read = sem("o_read")
        rden_set = sem("rden_set")
        job_full = [sem("job_full0"), sem("job_full1")]
        job_read = [sem("job_read0"), sem("job_read1")]
        split_step = sem("split_step")
        parts_set = [sem("parts_set0"), sem("parts_set1")]
        msplit_step = sem("msplit_step")
        mparts_set = sem("mparts_set")
        stack_placed = [sem(f"stack_placed{g}") for g in range(GROUPS)]
        max_placed = [sem(f"max_placed{g}") for g in range(GROUPS)]
        base_set = sem("base_set")
        xn_stored = sem("xn_stored")
        base_stored = sem("base_stored")
        t_set = sem("t_set")
        sink_dve, sink_act, sink_pe = sem("sink_dve"), sem("sink_act"), sem("sink_pe")
        route_const = sem("route_const")
        iota_set = sem("iota_set")
        gates_set = sem("gates_set")
        dve_chain = sem("dve_chain")
        sel_set = sem("sel_set")
        ranks_full = sem("ranks_full")
        posu_set = sem("posu_set")
        table_set = sem("table_set")
        pads_set = sem("pads_set")
        pad_placed = sem("pad_placed")
        beyond_placed = sem("beyond_placed")
        srow_loaded = [sem("srow_loaded0"), sem("srow_loaded1")]
        srow_set = [sem("srow_set0"), sem("srow_set1")]
        srow_placed = [sem("srow_placed0"), sem("srow_placed1")]
        up_loaded = sem("up_loaded")
        down_loaded = sem("down_loaded")
        tin_loaded = sem("tin_loaded")
        tinT_full, tinT_read = sem("tinT_full"), sem("tinT_read")
        g_full, g_read = sem("g_full"), sem("g_read")
        p_full, h_set = sem("p_full"), sem("h_set")
        hT_full, hT_read = sem("hT_full"), sem("hT_read")
        y_full, y_read = sem("y_full"), sem("y_read")
        meta_step = sem("meta_step")
        y_added = sem("y_added")
        y_read_meta = sem("y_read_meta")
        sc_rows = sc[:, :, :, :].rearrange("p t b e -> p (t b) e")
        ended = sem("ended")

        block = ctx.enter_context(nc.Block())

        def is_reg(v):
            return not isinstance(v, int)

        def wait(eng, s, v):
            if is_reg(v) or v > 0:
                eng.wait_ge(s, v)

        def wait_apart(eng, s, v):
            wait(eng, s, v)
            if is_reg(v):
                eng.sem_inc(passed, 1)

        def here(b, who):
            return True if is_reg(b) else present(b, who)

        def over_batches(eng, body):
            body(0)
            body(1)
            with eng.Fori(2, B - 1) as b:
                body(b)
            body(B - 1)
            body(B)

        def jobs(b, step, slot, engine=None, late=0):
            at = STEP * step + slot - late
            return [(n, a) for st, sl, n, a, e, who in MISC
                    if STEP * st + sl == at and engine in (None, e) and here(b, who)]

        def wait_job(eng, b, name, arg):
            wait(eng, job_full[bank_of(name, arg)], filled(b, name, arg))

        @block.tensor
        def _(pe):
            def mm(o, l, r, start=True, stop=True):
                return nc.tensor.matmul(o, l, r, start=start, stop=stop)

            pe.wait_ge(ident_set, 2)
            pe.wait_ge(w_loaded, 16 * 4)
            for m in range(4):
                for e in range(KT):
                    n = 2 * m + e
                    if n >= 2:
                        pe.wait_ge(w_copied, n - 1)
                    for f in range(2):
                        last = nc.tensor.transpose(s1[:, n % 2, f * P:(f + 1) * P],
                                                   wnat[:, m, f, e * P:(e + 1) * P], ident[:, :])
                    last.then_inc(w_turned, 1)
            pe.wait_ge(small_loaded, 16 * 12)
            pe.wait_ge(w_copied, 7)
            for e in range(KT):
                last = nc.tensor.transpose(s1[:, 0, e * NE:(e + 1) * NE], rw[:, e * P:(e + 1) * P], ident[0:NE, 0:NE])
            last.then_inc(w_turned, 1)
            pe.wait_ge(w_copied, 9)

            def job(b, name, arg):
                bank = bank_of(name, arg)
                o = misc[:, bank, :]
                wait(pe, job_read[bank], filled(b, name, arg) - 1)
                if name == "max_rows":
                    bb = b if same_batch(arg) else b - 1
                    pe.wait_ge(s1_read, bb * UNITS + STEP * (arg + 1))
                    for t in range(TT):
                        last = nc.tensor.transpose(o[0:GH, t * P:(t + 1) * P], mx[:, arg % 2, t, :], ident[:, :])
                elif name in ("q_proj", "k_proj"):
                    w = wqT if name == "q_proj" else wkT
                    bx = b if arg else b + 1
                    xb = b if arg == 0 else b - 1
                    if is_reg(b) or xb >= 0:
                        wait(pe, job_read[bank_of("x_cols", 0)], filled(xb, "x_cols", 0))
                        wait(pe, job_read[bank_of("x_cols", 1)], filled(xb, "x_cols", 1))
                    for e in range(KT):
                        last = mm(o, w[:, e, arg * P:(arg + 1) * P], xc[:, e, :], e == 0, e == KT - 1)
                elif name == "v_proj":
                    for t in range(TT):
                        for e in range(KT):
                            last = mm(o[:, t * P:(t + 1) * P], xc[:, e, t * P:(t + 1) * P],
                                      wvT[:, e, arg * P:(arg + 1) * P], e == 0, e == KT - 1)
                elif name == "x_cols":
                    pe.wait_ge(ln_done[0], (b + 2) * TT)
                    for t in range(TT):
                        last = nc.tensor.transpose(o[:, t * P:(t + 1) * P], xin[:, t, arg * P:(arg + 1) * P], ident[:, :])
                elif name == "out_rows":
                    bb = b if arg == 0 else b - 1
                    pe.wait_ge(o_read, bb * GROUPS + arg + 1)
                    for t in range(TT):
                        last = nc.tensor.transpose(o[:, t * P:(t + 1) * P], o32[:, t * P:(t + 1) * P], ident[:, :])
                elif name == "att_cols":
                    wait(pe, job_read[bank_of("out_rows", 3)], filled(b, "out_rows", 3))
                    for t in range(TT):
                        last = nc.tensor.transpose(o[:, t * P:(t + 1) * P], att[:, t, arg * P:(arg + 1) * P], ident[:, :])
                elif name == "att_out":
                    for k in range(KT):
                        wait(pe, job_read[bank_of("att_cols", k)], filled(b, "att_cols", k))
                    for t in range(2):
                        for k in range(KT):
                            last = mm(o[:, t * E:(t + 1) * E], attc[:, k, (2 * arg + t) * P:(2 * arg + t + 1) * P],
                                      woT[:, k, :], k == 0, k == KT - 1)
                elif name == "xn_cols":
                    pe.wait_ge(ln_done[1], b * TT)
                    for t in range(TT):
                        last = nc.tensor.transpose(o[:, t * P:(t + 1) * P], xn[:, t, arg * P:(arg + 1) * P], ident[:, :])
                elif name == "router":
                    for k in range(KT):
                        wait(pe, job_read[bank_of("xn_cols", k)], filled(b, "xn_cols", k))
                    for t in range(TT):
                        for k in range(KT):
                            last = mm(o[:, t * NE:(t + 1) * NE], xnc[:, k, t * P:(t + 1) * P], rwT[:, k, :],
                                      k == 0, k == KT - 1)
                last.then_inc(job_full[bank], 1)

            def score_max(b, g, s):
                n = b * UNITS + g * STEP + s
                h, t = GH * g + s // TT, s % TT
                if s == 0:
                    pe.wait_ge(stack_placed[g], (b + 1) * 16 * 2 * PAIRS)
                    if not is_reg(b) and b == 0:
                        pe.wait_ge(edges_placed, 16 * 7)
                wait(pe, s1_read, n - 1)
                mm(s1[:, s % 2, :], qst[0:MAX_ROW, h, t * P:(t + 1) * P], kst[0:MAX_ROW, h, :]).then_inc(s1_full, 1)

            def score_keys(b, g, u):
                n = b * UNITS + g * STEP + u
                h, t = GH * g + u % GH, u // GH
                if u == 0:
                    pe.wait_ge(max_placed[g], (b + 1) * 16 * 3)
                wait(pe, exp_done, n - {0: 1, 1: 4, 2: 4}.get(u, 3) + 1)
                mm(s2[:, u % 3, :], kst[0:SROWS, h, t * P:(t + 1) * P], qst[0:SROWS, h, :]).then_inc(s2_full, 1)

            def weigh_values(b, g, t):
                pe.wait_ge(exp_done, b * UNITS + g * STEP + GH * (t + 1))
                if t == 0:
                    wait(pe, o_read, b * GROUPS + g)
                    name = ("v_proj", g // 2)
                    vb = b
                    wait(pe, job_read[bank_of(*name)], filled(vb, *name))
                for j in range(GH):
                    last = mm(pv[32 * j:32 * j + 32, :], vau[:, t, GH * g + j, :], prob[:, t % 2, j, :],
                              t == 0, t == TT - 1)
                last.then_inc(pv_part, 1)

            def body(b):
                for step in range(GROUPS):
                    g2 = (step + 2) % GROUPS
                    b2 = b if step >= 2 else b - 1
                    g3 = (step + 1) % GROUPS
                    b3 = b if step >= 3 else b - 1
                    do2 = here(b, "cur" if step >= 2 else "prev")
                    do3 = here(b, "cur" if step >= 3 else "prev")
                    for s in range(STEP):
                        if here(b, "cur"):
                            score_max(b, step, s)
                        if do2:
                            score_keys(b2, g2, s)
                        if s == 2 and do3:
                            weigh_values(b3, g3, TT - 1)
                        if s in (6, 10, 14) and do2:
                            weigh_values(b2, g2, (s - 6) // 4)
                        for name, arg in jobs(b, step, s):
                            job(b, name, arg)

            pe.wait_ge(const_set, 2)
            for e in range(KT):
                pe.wait_ge(ln_done[0], TT)
                for t in range(TT):
                    last = nc.tensor.transpose(s1[:, e, t * P:(t + 1) * P], xin[:, t, e * P:(e + 1) * P], ident[:, :])
                last.then_inc(w_turned, 1)
            for qk in range(2):
                w = (wqT, wkT)[qk]
                pe.wait_ge(w_copied, 11)
                for e in range(KT):
                    last = mm(misc[:, qk, :], w[:, e, 0:P], xc[:, e, :], e == 0, e == KT - 1)
                last.then_inc(w_turned, 1)
            pe.wait_ge(w_copied, 13)
            over_batches(pe, body)

            for it in range(3):
                pe.wait_ge(sink_dve, 8 * it + 4)
                for t in range(TT):
                    last = nc.tensor.transpose(misc[:, 0, t * P:(t + 1) * P],
                                               sc[:, t, :, :].rearrange("p b e -> p (b e)"), ident[:, :])
                last.then_inc(sink_pe, 1)
                pe.wait_ge(sink_dve, 8 * it + 7)
                for t in range(TT):
                    last = nc.tensor.transpose(misc[:, 1, t * P:(t + 1) * P], colla[:, t * P:(t + 1) * P], ident[:, :])
                last.then_inc(sink_pe, 1)
            pe.wait_ge(sel_set, 1)
            pe.wait_ge(route_const, 3)
            both = work[:, :, :].rearrange("p j e -> p (j e)")
            mm(s1[:, 0, :], lower[:, :], both)
            mm(s1[:, 1, :], ones[:, :], both).then_inc(ranks_full, 1)

            tile_g, tile_p, tile_hT, tile_y, tile_t = s1[:, 0, :], s1[:, 1, :], s2[:, 0, :], s2[:, 1, 0:E], s2[:, 2, 0:KT * P]

            def turn_in(i):
                pe.wait_ge(tin_loaded, 16 * (i + 1))
                wait(pe, tinT_read, i)
                for e in range(KT):
                    last = nc.tensor.transpose(tile_t[:, e * P:(e + 1) * P], tin[:, e * P:(e + 1) * P], ident[:, :])
                last.then_inc(tinT_full, 1)

            def up(i, w, o, expert, full, read):
                pe.wait_ge(tinT_read, i + 1)
                wait(pe, read, i)
                for e in range(KT):
                    last = nc.tensor.matmul(o, tinT[:, e, :], w[:, bass.ds(expert * KT + e, 1), :],
                                            start=e == 0, stop=e == KT - 1)
                last.then_inc(full, 1)

            def turn_hidden(i):
                pe.wait_ge(h_set, i + 1)
                wait(pe, hT_read, i)
                for f in range(FT):
                    last = nc.tensor.transpose(tile_hT[:, f * P:(f + 1) * P], hsb[:, f * P:(f + 1) * P], ident[:, :])
                last.then_inc(hT_full, 1)

            def down(i, expert):
                pe.wait_ge(hT_read, i + 1)
                wait(pe, y_read, i)
                for f in range(FT):
                    last = nc.tensor.matmul(tile_y, hT[:, f, :], wos[:, bass.ds(expert * FT + f, 1), :],
                                            start=f == 0, stop=f == FT - 1)
                last.then_inc(y_full, 1)

            def tile(i, first=False, last=False):
                if not last:
                    expert = pe.value_load(tabu[0:1, 1, bass.ds(i, 1)], min_val=0, max_val=NE - 1)
                    up(i, wgs, tile_g, expert, g_full, g_read)
                if not first:
                    turn_hidden(i - 1)
                if not last:
                    up(i, wps, tile_p, expert, p_full, h_set)
                    if is_reg(i) or i < NT - 1:
                        turn_in(i + 1)
                if not first:
                    before = pe.value_load(tabu[0:1, 1, bass.ds(i - 1, 1)], min_val=0, max_val=NE - 1)
                    down(i - 1, before)

            pe.wait_ge(table_set, 1)
            pe.wait_ge(up_loaded, 32)
            turn_in(0)
            tile(0, first=True)
            pe.wait_ge(down_loaded, 16)
            tile(1)
            with pe.Fori(2, NT - 1) as i:
                tile(i)
            tile(NT - 1)
            tile(NT, last=True)

        @block.scalar
        def _(act):
            def copy(o, i):
                return nc.scalar.activation(o, i, ACT.Copy)

            for m in range(4):
                for e in range(KT):
                    n = 2 * m + e
                    act.wait_ge(w_turned, n + 1)
                    dst = (wqT, wkT, wvT, woT)[m][:, e, :]
                    src = s1[:, n % 2, 0:E]
                    if m < 2:
                        for q in range(4):
                            last = copy(dst[:, q * 64:(q + 1) * 64].rearrange("p (d h) -> p h d", h=GH),
                                        src[:, q * 64:(q + 1) * 64].rearrange("p (h d) -> p h d", h=GH))
                    else:
                        last = copy(dst, src)
                    last.then_inc(w_copied, 1)
            act.wait_ge(w_turned, 9)
            copy(rwT[:, :, :], s1[:, 0, 0:KT * NE].rearrange("p (k n) -> p k n", k=KT)).then_inc(w_copied, 1)
            act.wait_ge(small_loaded, 16 * 12)
            act.mul(bias[:, :, 0], bias[:, :, 0], SCALE).then_inc(bias_scaled, 1)
            act.wait_ge(bias_scaled, 1)
            for e in range(KT):
                act.wait_ge(w_turned, 10 + e)
                copy(xc[:, e, :], s1[:, e, :]).then_inc(w_copied, 1)

            def project_out(qk, m, src):
                scale = SCALE if qk == 0 else 1.0
                return nc.scalar.activation(qk32[:, qk, m, :], src, ACT.Identity, bias=bias[:, m, qk:qk + 1], scale=scale)

            for qk in range(2):
                act.wait_ge(w_turned, 12 + qk)
                project_out(qk, 0, misc[:, qk, :]).then_inc(w_copied, 1)

            def job(b, name, arg):
                bank = bank_of(name, arg)
                src = misc[:, bank, :]
                wait_job(act, b, name, arg)
                if name == "max_rows":
                    bb = b if same_batch(arg) else b - 1
                    wait(act, mparts_set, bb * GROUPS + arg)
                    last = nc.scalar.activation(negm[:, :], src[0:GH, :], ACT.Copy, scale=-1.0)
                elif name in ("q_proj", "k_proj"):
                    qk = 0 if name == "q_proj" else 1
                    n = b if arg else b + 1
                    wait(act, parts_set[arg], 2 * n)
                    last = project_out(qk, arg, src)
                elif name == "x_cols":
                    last_use = ("v_proj", 1)
                    wait(act, job_full[bank_of(*last_use)], filled(b, *last_use))
                    last = copy(xc[:, arg, :], src)
                elif name == "att_cols":
                    if is_reg(b) or b > 1:
                        prev = ("att_out", 1)
                        wait(act, job_full[bank_of(*prev)], filled(b - 1, *prev))
                    last = copy(attc[:, arg, :], src)
                elif name == "xn_cols":
                    if is_reg(b) or b > 1:
                        prev = ("router", 0)
                        wait(act, job_full[bank_of(*prev)], filled(b - 1, *prev))
                    last = copy(xnc[:, arg, :], src)
                last.then_inc(job_read[bank], 1)

            def exps(b, g, u):
                n = b * UNITS + g * STEP + u
                t = u // GH
                act.wait_ge(s2_full, n + 1)
                if u % GH == 0:
                    wait(act, pv_part, (b * GROUPS + g) * TT + t - 1)
                nc.scalar.activation(prob[:, t % 2, u % GH, :], s2[:, u % 3, :], ACT.Exp).then_inc(exp_done, 1)

            def outputs(b, g):
                n = b * GROUPS + g
                act.wait_ge(pv_part, (n + 1) * TT)
                pg = (g - 1) % GROUPS
                pb = b if g else b - 1
                it = pb + 1 if pg else pb
                if is_reg(n) or n > 0:
                    wait(act, job_full[bank_of("out_rows", pg)], filled(it, "out_rows", pg))
                copy(o32[:, :], pv[:, :]).then_inc(o_read, 1)

            def body(b):
                for step in range(GROUPS):
                    g2 = (step + 2) % GROUPS
                    b2 = b if step >= 2 else b - 1
                    g3 = (step + 1) % GROUPS
                    b3 = b if step >= 3 else b - 1
                    for s in range(STEP):
                        if here(b, "cur" if step >= 2 else "prev"):
                            exps(b2, g2, s)
                        if s == 3 and here(b, "cur" if step >= 3 else "prev"):
                            outputs(b3, g3)
                        for name, arg in jobs(b, step, s, "act", late=1):
                            job(b, name, arg)

            over_batches(act, body)

            for it in range(3):
                act.wait_ge(sink_dve, 8 * it + 2)
                nc.scalar.activation(gates[:, :, :], sc_rows, ACT.Exp).then_inc(sink_act, 1)
                act.wait_ge(sink_dve, 8 * it + 3)
                nc.scalar.activation(rowl[:, :], rowm[:, :], ACT.Ln).then_inc(sink_act, 1)
                act.wait_ge(sink_dve, 8 * it + 6)
                nc.scalar.activation(attc[:, 0, :], misc[:, 0, :], ACT.Exp, bias=colm[:, 1:2],
                                     accum_out=colm[:, 2:3]).then_inc(sink_act, 1)
                act.wait_ge(sink_act, 4 * it + 3)
                nc.scalar.activation(colm[:, 3:4], colm[:, 2:3], ACT.Ln).then_inc(sink_act, 1)
            act.wait_ge(sink_dve, 8 * 3)
            nc.scalar.activation(gates[:, :, :], sc_rows, ACT.Exp).then_inc(gates_set, 1)

            def tile(i, first=False, last=False):
                if not last:
                    act.wait_ge(g_full, i + 1)
                    wait(act, h_set, i)
                    nc.scalar.activation(gsb[:, :], s1[:, 0, :], ACT.Relu).then_inc(g_read, 1)
                if not first:
                    act.wait_ge(hT_full, i)
                    wait(act, y_full, i - 1)
                    copy(hT[:, :, :], s2[:, 0, :].rearrange("p (f n) -> p f n", f=FT)).then_inc(hT_read, 1)

            tile(0, first=True)
            tile(1)
            with act.Fori(2, NT) as i:
                tile(i)
            tile(NT, last=True)

        @block.vector
        def _(dve):
            nc.vector.memset(vau[:, :, :, D:2 * D], 1.0).then_inc(const_set, 1)
            nc.vector.memset(nhalf[:, :], -0.5).then_inc(const_set, 1)

            def ln_statistics(which, src, b, tiles):
                if 0 in tiles:
                    wait(dve, ln_done[which], b * TT)
                for t in tiles:
                    nc.vector.bn_stats(stats[:, which, t, :], src[:, t, :]).then_inc(ln_stats[which], 1)

            def ln_means(which, b):
                for t in range(TT):
                    wait_apart(dve, ln_stats[which], b * TT + t + 1)
                    nc.vector.bn_aggr(mv[:, which, t, :], stats[:, which, t, :]).then_inc(ln_mean[which], 1)

            def ln_apply(which, dst, src, b, tiles):
                dve.wait_ge(ln_rstd[which], b + 1)
                for t in tiles:
                    nc.vector.tensor_scalar(dst[:, t, :], src[:, t, :], mv[:, which, t, 0:1], rstd[:, which, t:t + 1],
                                            ALU.subtract, ALU.mult).then_inc(ln_done[which], 1)

            def job(b, name, arg):
                bank = bank_of(name, arg)
                src = misc[:, bank, :]
                wait_job(dve, b, name, arg)
                if name == "v_proj":
                    wait(dve, pv_part, ((b - 1) * GROUPS + 2 * arg + 2) * TT)
                    last = nc.vector.tensor_tensor(
                        vau[:, :, 8 * arg:8 * arg + 8, 0:D],
                        src.rearrange("p (t h d) -> p t h d", t=TT, h=8),
                        bvb[:, arg * P:(arg + 1) * P].rearrange("p (h d) -> p h d", h=8).unsqueeze(1)
                        .broadcast_to([P, TT, 8, D]), ALU.add)
                elif name == "out_rows":
                    bb = b if arg == 0 else b - 1
                    rows = src.rearrange("p (t h d) -> p t h d", t=TT, h=GH)
                    pa, it = (arg - 1) % GROUPS, (b - 1 if arg == 1 else b)
                    if is_reg(b) or b > 1 or (arg, b) not in ((0, 0),):
                        wait(dve, job_read[bank_of("out_rows", pa)], filled(it, "out_rows", pa))
                    nc.vector.reciprocal(rden[:, :, :], rows[:, :, :, D]).then_inc(rden_set, 1)
                    dve.wait_ge(rden_set, bb * GROUPS + arg + 1)
                    if arg == 0 and (is_reg(bb) or bb > 0):
                        prev = ("att_cols", 1)
                        for k in range(KT):
                            wait(dve, job_full[bank_of("att_cols", k)], filled(b, "att_cols", k))
                    last = nc.vector.tensor_tensor(
                        att[:, :, arg * GH * D:(arg + 1) * GH * D].rearrange("p t (h d) -> p t h d", h=GH),
                        rows[:, :, :, 0:D],
                        rden[:, :, :].unsqueeze(3).broadcast_to([P, TT, GH, D]), ALU.mult)
                elif name == "att_out":
                    if arg == 0:
                        dve.wait_ge(xres_loaded, 16 * b)
                    last = nc.vector.tensor_tensor(xres[:, 2 * arg:2 * arg + 2, :],
                                                   src.rearrange("p (t e) -> p t e", t=2),
                                                   xres[:, 2 * arg:2 * arg + 2, :], ALU.add)
                elif name == "router":
                    last = nc.vector.tensor_tensor(sc[:, :, bass.ds(b - 1, 1), :],
                                                   src[:, 0:TT * NE].rearrange("p (t o n) -> p t o n", t=TT, o=1),
                                                   rbb[:, :].unsqueeze(1).unsqueeze(1).broadcast_to([P, TT, 1, NE]), ALU.add)
                last.then_inc(job_read[bank], 1)

            def maxima(b, g, s):
                n = b * UNITS + g * STEP + s
                if s == 0:
                    pg, it = (g - 2) % GROUPS, b
                    if g == 0:
                        it = b - 1
                    elif g == 1:
                        it = b
                    if is_reg(b) or b > 0 or g >= 2:
                        wait(dve, job_full[bank_of("max_rows", pg)], filled(it, "max_rows", pg))
                dve.wait_ge(s1_full, n + 1)
                nc.vector.tensor_reduce(mx[:, g % 2, s % TT, s // TT:s // TT + 1], s1[:, s % 2, :], AX_X, ALU.max)\
                    .then_inc(s1_read, 1)

            def body(b):
                for step in range(GROUPS):
                    for s in range(STEP):
                        if here(b, "cur"):
                            maxima(b, step, s)
                        at = (step, s)
                        if here(b, "next"):
                            if at == (0, 5):
                                dve.wait_ge(x_loaded, 16 * (b + 2))
                            if at in ((0, 5), (0, 7)):
                                ln_statistics(0, xin, b + 1, ((0, 1) if s == 5 else (2, 3)))
                            if at == (0, 9):
                                ln_means(0, b + 1)
                            if at in ((1, 2), (1, 4)):
                                ln_apply(0, xin, xin, b + 1, ((0, 1) if s == 2 else (2, 3)))
                        if here(b, "prev"):
                            if at in ((3, 3), (3, 4)):
                                i = s - 3
                                wait(dve, job_read[bank_of("att_out", i)], filled(b, "att_out", i))
                                ln_statistics(1, xres, b - 1, (2 * i, 2 * i + 1))
                            if at == (3, 5):
                                ln_means(1, b - 1)
                            if at == (3, 7):
                                if is_reg(b) or b > 1:
                                    dve.wait_ge(xn_stored, 16 * (b - 1))
                                    dve.wait_ge(base_set, b - 1)
                                    wait(dve, job_full[bank_of("xn_cols", 1)], filled(b - 1, "xn_cols", 1))
                                ln_apply(1, xn, xres, b - 1, range(TT))
                        for name, arg in jobs(b, step, s, "dve", late=1):
                            job(b, name, arg)

            dve.wait_ge(small_loaded, 16 * 12)
            dve.wait_ge(x_loaded, 16)
            ln_statistics(0, xin, 0, range(TT))
            ln_means(0, 0)
            ln_apply(0, xin, xin, 0, range(TT))
            over_batches(dve, body)

            count = [0]

            def link(ins):
                count[0] += 1
                ins.then_inc(dve_chain, 1)
                dve.wait_ge(dve_chain, count[0])

            def along(a, n=NE):
                return a.unsqueeze(2).broadcast_to([P, J, n])

            def per_expert(a):
                return a.unsqueeze(1).broadcast_to([P, J, NE])

            tt, ts, red = nc.vector.tensor_tensor, nc.vector.tensor_scalar, nc.vector.tensor_reduce
            link(ts(tinv[:, :], tmp1[:, :], 0.1, None, ALU.max))
            link(nc.vector.reciprocal(tinv[:, :], tinv[:, :]))
            wait(dve, job_read[bank_of("router", 0)], filled(B, "router", 0))
            link(ts(sc_rows, sc_rows, tinv[:, 0:1], None, ALU.mult))
            for it in range(3):
                red(rowl[:, :], sc_rows, AX_X, ALU.max).then_inc(sink_dve, 1)
                dve.wait_ge(sink_dve, 8 * it + 1)
                tt(sc_rows, sc_rows, along(rowl[:, :]), ALU.subtract).then_inc(sink_dve, 1)
                dve.wait_ge(sink_act, 4 * it + 1)
                red(rowm[:, :], gates[:, :, :], AX_X, ALU.add).then_inc(sink_dve, 1)
                dve.wait_ge(sink_act, 4 * it + 2)
                tt(sc_rows, sc_rows, along(rowl[:, :]), ALU.subtract).then_inc(sink_dve, 1)
                dve.wait_ge(sink_pe, 2 * it + 1)
                red(colm[:, 0:1], misc[:, 0, :], AX_X, ALU.max).then_inc(sink_dve, 1)
                dve.wait_ge(sink_dve, 8 * it + 5)
                ts(colm[:, 1:2], colm[:, 0:1], -1.0, None, ALU.mult).then_inc(sink_dve, 1)
                dve.wait_ge(sink_act, 4 * it + 4)
                ts(colla, misc[:, 0, :], colm[:, 1:2], colm[:, 3:4], ALU.add, ALU.subtract).then_inc(sink_dve, 1)
                dve.wait_ge(sink_pe, 2 * it + 2)
                nc.vector.tensor_copy(sc[:, :, :, :].rearrange("p t b e -> p (t b e)"), misc[:, 1, :]).then_inc(sink_dve, 1)
                dve.wait_ge(sink_dve, 8 * it + 8)
            dve.wait_ge(gates_set, 1)
            link(red(rowm[:, :], gates[:, :, :], AX_X, ALU.add))
            link(ts(rowm[:, :], rowm[:, :], 1e-8, None, ALU.add))
            link(nc.vector.reciprocal(rowm[:, :], rowm[:, :]))
            link(tt(gates[:, :, :], gates[:, :, :], along(rowm[:, :]), ALU.mult))
            dve.wait_ge(route_const, 3)
            for c in range(TOP):
                g = gates[:, :, :]
                if c:
                    link(nc.vector.scalar_tensor_tensor(out=g, in0=sel[:, 0, :, :], scalar=-4.0, in1=g,
                                                        op0=ALU.mult, op1=ALU.add))
                link(red(topv[:, c, :], g, AX_X, ALU.max))
                link(tt(work[:, :, :], g, along(topv[:, c, :]), ALU.is_equal))
                link(tt(work[:, :, :], work[:, :, :], per_expert(rev[:, :]), ALU.mult))
                link(red(rowl[:, :], work[:, :, :], AX_X, ALU.max))
                link(tt(sel[:, c, :, :], along(rowl[:, :]), per_expert(rev[:, :]), ALU.is_equal))
            tt(work[:, :, :], sel[:, 0, :, :], sel[:, 1, :, :], ALU.add).then_inc(sel_set, 1)
            link(tt(rowm[:, :], topv[:, 0, :], topv[:, 1, :], ALU.add))
            link(ts(rowm[:, :], rowm[:, :], 1e-8, None, ALU.add))
            link(nc.vector.reciprocal(rowm[:, :], rowm[:, :]))
            for c in range(TOP):
                link(tt(topv[:, c, :], topv[:, c, :], rowm[:, :], ALU.mult))
            dve.wait_ge(ranks_full, 1)
            here_n = s1[:, 1, :].rearrange("p (j e) -> p j e", e=NE)
            for e in range(NE):
                link(nc.vector.tensor_tensor_scan(gates[:, :, e], ones[:, 0:J], here_n[:, :, e], 0.0, ALU.mult, ALU.add))
            link(nc.vector.tensor_copy(padf[:, :], gates[:, J - 1, :]))
            link(tt(work[:, :, :], gates[:, :, :], here_n, ALU.subtract))
            link(tt(work[:, :, :], work[:, :, :], s1[:, 0, :].rearrange("p (j e) -> p j e", e=NE), ALU.add))
            link(tt(work[:, :, :], work[:, :, :], per_expert(regoff[:, :]), ALU.add))
            for c in range(TOP):
                link(tt(sel[:, c, :, :], sel[:, c, :, :], work[:, :, :], ALU.mult))
                link(red(posf[:, :], sel[:, c, :, :], AX_X, ALU.add))
                link(nc.vector.tensor_copy(posu[:, c, :], posf[:, :]))
            n_e = padf[0:1, :]
            link(tt(cmp1, n_e.unsqueeze(2).broadcast_to([1, NE, J]), kk[:, :].unsqueeze(1).broadcast_to([1, NE, J]),
                    ALU.is_gt))
            link(red(tiles[:, 0, :], cmp1, AX_X, ALU.add))
            link(nc.vector.tensor_tensor_scan(tiles[:, 1, :], ones[0:1, 0:NE], tiles[:, 0, :], 0.0, ALU.mult, ALU.add))
            over_e = [1, NT, NE]
            link(tt(cmp2, ti[:, :].unsqueeze(2).broadcast_to(over_e), tiles[:, 1, :].unsqueeze(1).broadcast_to(over_e),
                    ALU.is_ge))
            link(tt(cmp3, cmp2, tiles[:, 0, :].unsqueeze(1).broadcast_to(over_e), ALU.mult))
            link(red(tabf[:, 0, :], cmp2, AX_X, ALU.add))
            link(red(tabf[:, 1, :], cmp3, AX_X, ALU.add))
            link(tt(tabf[:, 1, :], ti[:, :], tabf[:, 1, :], ALU.subtract))
            link(ts(tabf[:, 1, :], tabf[:, 1, :], float(P), None, ALU.mult))
            link(ts(tabf[:, 2, :], tabf[:, 0, :], float(REGION), None, ALU.mult))
            link(tt(tabf[:, 1, :], tabf[:, 1, :], tabf[:, 2, :], ALU.add))
            link(ts(tabf[:, 0, :], tabf[:, 0, :], float(NE - 1), None, ALU.min))
            link(nc.vector.tensor_copy(tabu[:, 1, :], tabf[:, 0, :]))
            nc.vector.tensor_copy(tabu[:, 0, :], tabf[:, 1, :]).then_inc(table_set, 1)
            link(tt(padf[:, :], padf[:, :], regoff[:, :], ALU.add))
            link(ts(padf[:, :], padf[:, :], pidx[:, 0:1], None, ALU.add))
            nc.vector.tensor_copy(padu[:, :], padf[:, :]).then_inc(pads_set, 1)
            dve.wait_ge(pads_set, 1)

            def fill_rows(n, k):
                b = n * 2 + k
                dve.wait_ge(srow_loaded[k], 16 * (n + 1))
                for c in range(TOP):
                    if c:
                        nc.vector.tensor_copy(srow[:, k, 1, :, 0:E], srow[:, k, 0, :, 0:E]).then_inc(srow_set[k], 1)
                    nc.vector.tensor_copy(srow[:, k, c, :, E:E + 1], by_batch(tokf, b)).then_inc(srow_set[k], 1)
                    nc.vector.tensor_copy(srow[:, k, c, :, E + 1:E + 2], by_batch(topv[:, c, :], b)).then_inc(srow_set[k], 1)
                    nc.vector.tensor_copy(sidx[:, k, c, :].unsqueeze(2), by_batch(posu[:, c, :], b)).then_inc(srow_set[k], 1)

            def by_batch(a, b):
                return a.rearrange("p (t b) -> p t b", t=TT)[:, :, bass.ds(b, 1)]

            def fill_pair(n):
                for k in range(2):
                    fill_rows(n, k)

            fill_pair(0)
            with dve.Fori(1, B // 2) as n:
                fill_pair(n)

            def turn_out(i):
                dve.wait_ge(tinT_full, i + 1)
                nc.vector.tensor_copy(tinT[:, :, :], s2[:, 2, 0:KT * P].rearrange("p (k n) -> p k n", k=KT))\
                    .then_inc(tinT_read, 1)

            def tile(i, first=False, last=False):
                if not last:
                    dve.wait_ge(p_full, i + 1)
                    dve.wait_ge(g_read, i + 1)
                    wait(dve, hT_full, i)
                    tt(hsb[:, :], gsb[:, :], s1[:, 1, :], ALU.mult).then_inc(h_set, 1)
                    if is_reg(i) or i < NT - 1:
                        turn_out(i + 1)
                if not first:
                    dve.wait_ge(y_full, i)
                    wait(dve, y_added, 16 * (i - 1))
                    nc.vector.tensor_copy(yidx[:, :], meta[:, 1, 0:1]).then_inc(y_read_meta, 1)
                    ts(ysb[:, :], s2[:, 1, 0:E], meta[:, 1, 1:2], None, ALU.mult).then_inc(y_read, 1)
                    dve.wait_ge(y_read, i)
                if not last:
                    nc.vector.tensor_copy(meta[:, 1, :], meta[:, 0, :]).then_inc(meta_step, 1)
                    dve.wait_ge(meta_step, 2 * i + 2)
                    if is_reg(i) or i < NT - 1:
                        nc.vector.tensor_copy(meta[:, 0, :], tin[:, E:E + 2]).then_inc(meta_step, 1)
                        dve.wait_ge(meta_step, 2 * i + 3)

            turn_out(0)
            nc.vector.tensor_copy(meta[:, 0, :], tin[:, E:E + 2]).then_inc(meta_step, 1)
            dve.wait_ge(meta_step, 1)
            tile(0, first=True)
            tile(1)
            with dve.Fori(2, NT - 1) as i:
                tile(i)
            tile(NT - 1)
            tile(NT, last=True)

        @block.gpsimd
        def _(pool):
            nc.gpsimd.memset(ident[:, :], 0.0).then_inc(ident_set, 1)
            pool.wait_ge(ident_set, 1)
            nc.gpsimd.affine_select(out=ident[:, :], in_=ident[:, :], compare_op=ALU.not_equal, fill=1.0, base=0,
                                    pattern=[[-1, P]], channel_multiplier=1).then_inc(ident_set, 1)
            nc.gpsimd.memset(edge[:, :, :], 0.0).then_inc(edge_set, 1)
            pool.wait_ge(edge_set, 1)
            nc.gpsimd.memset(edge[:, K_LAST, N - 1:N], 1.0).then_inc(edge_set, 1)
            nc.gpsimd.memset(edge[:, K_FIRST, 0:1], 1.0).then_inc(edge_set, 1)
            nc.gpsimd.memset(edge[:, ONES, :], 1.0).then_inc(edge_set, 1)
            nc.gpsimd.memset(edge[:, Q_FIRST, 0:1], NEG).then_inc(edge_set, 1)
            nc.gpsimd.memset(edge[:, Q_LAST, N - 1:N], NEG).then_inc(edge_set, 1)

            def rsqrt(which, b):
                wait_apart(pool, ln_mean[which], TT * (b + 1))
                nc.gpsimd.tensor_scalar(varp[:, which, :], mv[:, which, :, 1], LN_EPS, None, ALU.add)\
                    .then_inc(ln_varp[which], 1)
                wait_apart(pool, ln_varp[which], b + 1)
                nc.gpsimd.tensor_tensor(rstd[:, which, :], varp[:, which, :], nhalf[:, :], ALU.pow)\
                    .then_inc(ln_rstd[which], 1)

            def split(value, left, out_parts, step_sem, done, n):
                hi, mid, lo = (out_parts[:, i, :] for i in range(3))
                nc.gpsimd.tensor_copy(hi, value).then_inc(step_sem, 1)
                wait_apart(pool, step_sem, 3 * n + 1)
                nc.gpsimd.tensor_tensor(left, value, hi, ALU.subtract).then_inc(step_sem, 1)
                wait_apart(pool, step_sem, 3 * n + 2)
                nc.gpsimd.tensor_copy(mid, left).then_inc(step_sem, 1)
                wait_apart(pool, step_sem, 3 * n + 3)
                nc.gpsimd.tensor_tensor(lo, left, mid, ALU.subtract).then_inc(done, 1)

            def split_qk(b, m, qk):
                if qk == 0:
                    for g in (2 * m, 2 * m + 1):
                        wait_apart(pool, stack_placed[g], b * 16 * 2 * PAIRS)
                n = 4 * b + 2 * m + qk
                if is_reg(n) or n > 0:
                    if qk == 1:
                        wait_apart(pool, parts_set[m], 2 * b + 1)
                    elif m == 1:
                        wait_apart(pool, parts_set[0], 2 * b + 2)
                    else:
                        wait_apart(pool, parts_set[1], 2 * b)
                split(qk32[:, qk, m, :], rest[:, :], parts[:, m, qk, :, :], split_step, parts_set[m], n)

            def split_max(b, g):
                n = GROUPS * b + g
                if is_reg(n) or n > 0:
                    pg, pb = (g - 1) % GROUPS, (b if g else b - 1)
                    wait_apart(pool, max_placed[pg], (pb + 1) * 16 * 3)
                it = b + 1 if g == 3 else b
                wait_apart(pool, job_read[bank_of("max_rows", g)], filled(it, "max_rows", g))
                split(negm[:, :], mrest[:, :], mparts[:, :, :], msplit_step, mparts_set, n)

            pool.wait_ge(const_set, 2)
            rsqrt(0, 0)
            for qk in range(2):
                pool.wait_ge(w_copied, 12 + qk)
                split_qk(0, 0, qk)

            def body(b):
                for step in range(GROUPS):
                    if step == 0:
                        if here(b, "prev"):
                            split_max(b - 1, 3)
                        if here(b, "cur"):
                            for qk, name in enumerate(("q_proj", "k_proj")):
                                wait_apart(pool, job_read[bank_of(name, 1)], filled(b, name, 1))
                                split_qk(b, 1, qk)
                        if here(b, "next"):
                            rsqrt(0, b + 1)
                    elif here(b, "cur"):
                        split_max(b, step - 1)
                    if step == 2 and here(b, "next"):
                        wait_apart(pool, job_read[bank_of("q_proj", 0)], filled(b, "q_proj", 0))
                        split_qk(b + 1, 0, 0)
                        wait_apart(pool, job_read[bank_of("k_proj", 0)], filled(b, "k_proj", 0))
                        split_qk(b + 1, 0, 1)
                    if step == 3 and here(b, "prev"):
                        rsqrt(1, b - 1)
                        wait_apart(pool, ln_done[1], TT * b)
                        nc.gpsimd.tensor_tensor(xres[:, :, :], xres[:, :, :], xn[:, :, :], ALU.add).then_inc(base_set, 1)

            nc.gpsimd.memset(ones[:, :], 1.0).then_inc(route_const, 1)
            nc.gpsimd.memset(padrow[:, :], 0.0).then_inc(route_const, 1)
            pool.wait_ge(route_const, 2)
            nc.gpsimd.affine_select(out=lower[:, :], in_=ones[:, :], compare_op=ALU.is_gt, fill=0.0, base=0,
                                    pattern=[[1, P]], channel_multiplier=-1).then_inc(route_const, 1)
            for o, pattern, base, mult in (
                    (tokf[:, :], [[P, TT], [N, B]], 0, 1), (rev[:, :], [[-1, NE]], NE, 0),
                    (regoff[:, :], [[REGION, NE]], 0, 0), (pidx[:, :], [[1, 1]], 0, 1),
                    (kk[:, :], [[P, J]], 0, 0), (ti[:, :], [[1, NT]], 0, 0),
                    (padrow[:, E:E + 1], [[1, 1]], B * N, 1)):
                nc.gpsimd.iota(o, pattern=pattern, base=base, channel_multiplier=mult,
                                  allow_small_or_imprecise_dtypes=True).then_inc(iota_set, 1)

            over_batches(pool, body)

            pool.wait_ge(pads_set, 1)
            pool.wait_ge(iota_set, 7)
            for e in range(NE):
                nc.gpsimd.indirect_dma_start(slots_d, bass.IndirectOffsetOnAxis(ap=padu[:, e:e + 1], axis=0),
                                             padrow[:, :], None).then_inc(pad_placed, 16)

            def scatter_pair(n):
                for k in range(2):
                    wait_apart(pool, srow_set[k], 7 * (n + 1))
                    for c in range(TOP):
                        for t in range(TT):
                            nc.gpsimd.indirect_dma_start(
                                slots_d, bass.IndirectOffsetOnAxis(ap=sidx[:, k, c, t:t + 1], axis=0),
                                srow[:, k, c, t, :], None).then_inc(srow_placed[k], 16)

            scatter_pair(0)
            with pool.Fori(1, B // 2) as n:
                scatter_pair(n)

            def add(i):
                wait_apart(pool, y_read, i + 1)
                wait_apart(pool, y_read_meta, i + 1)
                wait_apart(pool, y_added, 16 * i)
                nc.gpsimd.indirect_dma_start(out, bass.IndirectOffsetOnAxis(ap=yidx[:, :], axis=0), ysb[:, :], None,
                                             compute_op=ALU.add).then_inc(y_added, 16)

            pool.wait_ge(base_stored, 16 * (B + 1))
            add(0)
            with pool.Fori(1, NT) as i:
                add(i)
            pool.wait_ge(y_added, 16 * NT)

        @block.sync
        def _(sp):
            def rows(t, b):
                return t[bass.ds(b * N, N), :].rearrange("(t p) e -> p t e", p=P)

            x_flat = x.rearrange("b n e -> (b n) e")
            for m, w in enumerate((Wq, Wk, Wv, Wo)):
                sp.dma_start(wnat[:, m, :, :], w.rearrange("(f p) e -> p f e", p=P)).then_inc(w_loaded, 16)
            sp.dma_start(xin[:, :, :], rows(x_flat, 0)).then_inc(x_loaded, 16)
            for qk, bb in enumerate((bq, bk)):
                for q in range(4):
                    src = bb[q * 64:(q + 1) * 64].rearrange("(h d o) -> d h o", h=GH, o=1)
                    with nc.allow_non_contiguous_dma("64 single biases"):
                        sp.dma_start(bias[64 * (q % 2):64 * (q % 2) + 64, q // 2, qk:qk + 1], src)\
                            .then_inc(small_loaded, 16)
            sp.dma_start(rw[:, :], router_w).then_inc(small_loaded, 16)
            with nc.allow_non_contiguous_dma("rows for all partitions"):
                sp.dma_start(bvb[:, :], bv.unsqueeze(0).broadcast_to([P, E])).then_inc(small_loaded, 16)
                sp.dma_start(rbb[:, :], router_b.unsqueeze(0).broadcast_to([P, NE])).then_inc(small_loaded, 16)
                sp.dma_start(tmp1[:, :], temperature.unsqueeze(0).broadcast_to([P, 1])).then_inc(small_loaded, 16)
            sp.wait_ge(edge_set, 6)
            for dst, row, src in ((kst, MASK_ROW, K_LAST), (kst, MASK_ROW + 1, K_FIRST), (kst, MAX_ROW, ONES),
                                  (kst, MAX_ROW + 1, ONES), (kst, MAX_ROW + 2, ONES),
                                  (qst, MASK_ROW, Q_FIRST), (qst, MASK_ROW + 1, Q_LAST)):
                sp.dma_start(dst[row:row + 1, :, :], edge[:, src, :].unsqueeze(1).broadcast_to([1, H, N]))\
                    .then_inc(edges_placed, 16)

            def place_stack(b, g):
                m, half = g // 2, g % 2
                wait_apart(sp, parts_set[m], 2 * (b + 1))
                wait_apart(sp, s2_full, (b - 1) * UNITS + (g + 1) * STEP)
                for qk, (dst, pick) in enumerate(((qst, Q_PART), (kst, K_PART))):
                    for c in range(PAIRS):
                        sp.dma_start(dst[c * D:(c + 1) * D, GH * g:GH * (g + 1), :],
                                     parts[64 * half:64 * half + 64, m, qk, pick[c], :]).then_inc(stack_placed[g], 16)

            def place_max(b, g):
                wait_apart(sp, mparts_set, b * GROUPS + g + 1)
                for i in range(3):
                    sp.dma_start(qst[MAX_ROW + i:MAX_ROW + i + 1, GH * g:GH * (g + 1), :], mparts[:, i, :])\
                        .then_inc(max_placed[g], 16)

            def body(b):
                if here(b, "next"):
                    if is_reg(b) or b > 0:
                        wait_apart(sp, job_full[bank_of("x_cols", 1)], filled(b - 1, "x_cols", 1))
                    else:
                        sp.wait_ge(w_turned, 11)
                    sp.dma_start(xin[:, :, :], rows(x_flat, b + 1)).then_inc(x_loaded, 16)
                if here(b, "cur"):
                    place_stack(b, 1)
                if here(b, "prev"):
                    place_max(b - 1, 3)
                if here(b, "cur"):
                    place_stack(b, 2)
                    place_max(b, 0)
                    place_stack(b, 3)
                    place_max(b, 1)
                if here(b, "prev"):
                    wait_apart(sp, base_stored, 16 * b)
                    sp.dma_start(xres[:, :, :], rows(x_flat, b - 1)).then_inc(xres_loaded, 16)
                if here(b, "next"):
                    place_stack(b + 1, 0)
                if here(b, "cur"):
                    place_max(b, 2)
                if here(b, "prev"):
                    wait_apart(sp, ln_done[1], TT * b)
                    sp.dma_start(rows(xn_d, b - 1), xn[:, :, :]).then_inc(xn_stored, 16)
                    wait_apart(sp, base_set, b)
                    sp.dma_start(rows(out, b - 1), xres[:, :, :]).then_inc(base_stored, 16)

            place_stack(0, 0)
            sp.dma_start(wgs[:, :, :], wg.rearrange("n (k p) f -> p (n k) f", p=P)).then_inc(up_loaded, 16)
            sp.dma_start(wps[:, :, :], wp.rearrange("n (k p) f -> p (n k) f", p=P)).then_inc(up_loaded, 16)
            sp.wait_ge(iota_set, 7)
            for i in range(8):
                sp.dma_start(slots_d[NE * REGION + i * P:NE * REGION + (i + 1) * P, :], padrow[:, :]).then_inc(beyond_placed, 16)
            sp.dma_start(out[B * N:B * N + P, :], padrow[:, 0:E]).then_inc(base_stored, 16)
            over_batches(sp, body)
            sp.wait_ge(s2_full, B * UNITS)
            sp.dma_start(wos, wo.rearrange("n (f p) e -> p (n f) e", p=P)).then_inc(down_loaded, 16)
            sp.wait_ge(xn_stored, 16 * B)

            def load_rows(n):
                for k in range(2):
                    wait_apart(sp, srow_placed[k], 16 * TOP * TT * n)
                    sp.dma_start(srow[:, k, 0, :, 0:E], rows(xn_d, n * 2 + k)).then_inc(srow_loaded[k], 16)

            sp.wait_ge(pv_part, B * GROUPS * TT)
            load_rows(0)
            with sp.Fori(1, B // 2) as n:
                load_rows(n)
            for k in range(2):
                sp.wait_ge(srow_placed[k], 16 * TOP * TT * B // 2)
            sp.wait_ge(pad_placed, 16 * NE)
            sp.wait_ge(beyond_placed, 16 * 8)
            sp.wait_ge(table_set, 1)

            def load_tile(i):
                if is_reg(i) or i > 0:
                    wait_apart(sp, tinT_full, i)
                    wait_apart(sp, meta_step, 2 * i - 1)
                slot = sp.value_load(tabu[0:1, 0, bass.ds(i, 1)], min_val=0, max_val=slots_d.shape[0] - P)
                sp.dma_start(tin[:, :], slots_d[bass.ds(slot, P), :]).then_inc(tin_loaded, 16)

            load_tile(0)
            with sp.Fori(1, NT) as i:
                load_tile(i)
            sp.wait_ge(base_stored, 16 * (B + 1))
            sp.wait_ge(y_added, 16 * NT)


_INS = ["x", "Wq", "bq", "Wk", "bk", "Wv", "bv", "Wo"]
_FFN = ["router_w", "router_b", "temperature", "wg", "wp", "wo"]


def kernel(**inputs):
    import numpy as _np
    import concourse.bacc as _bacc
    from concourse import mybir as _mybir
    from concourse.bass_utils import run_bass_kernel_spmd as _run

    nc = _bacc.Bacc("TRN2", target_bir_lowering=False, num_devices=1)
    arrays, args = {}, []
    for name in ["L0_attn_" + n for n in _INS] + ["L0_ffn_" + n for n in _FFN]:
        a = _np.ascontiguousarray(inputs[name])
        arrays[f"in_{name}"] = a
        args.append(nc.dram_tensor(f"in_{name}", a.shape, _mybir.dt.from_np(a.dtype), kind="ExternalInput").ap())
    shape = inputs["L0_attn_x"].shape
    tokens = shape[0] * shape[1]
    args.append(nc.dram_tensor("out_0", (tokens + P, shape[2]), _mybir.dt.float32, kind="ExternalOutput").ap())
    build(nc, *args)
    r = _run(nc, [arrays], core_ids=[0])
    return r.results[0]["out_0"][:tokens].reshape(shape)
```

```python
from contextlib import ExitStack

import concourse.bass as bass
from concourse import mybir

ALU = mybir.AluOpType
ACT = mybir.ActivationFunctionType
AX_X = mybir.AxisListType.X
F32 = mybir.dt.float32
U32 = mybir.dt.uint32
BF16 = mybir.dt.bfloat16

P = 128
NEG = -1.0e9
LN_EPS = 1e-5

Q_PART = (0, 0, 1, 0, 2, 1)
K_PART = (0, 1, 0, 2, 0, 1)
PAIRS = len(Q_PART)

BATCHES = 16

MISC = [
    ("max_rows", 3, 1, "act", "prev", (3,)),
    ("q_proj", 1, 0, "act", "cur", (0, 1, 3, 4)),
    ("xn_cols", 0, 1, "act", "routed", (6,)),
    ("xn_cols", 1, 0, "act", "routed", (7,)),
    ("router", 0, 1, "dve", "routed", (10, 11)),
    ("out_rows", 1, 1, "dve", "prev", (15,)),
    ("k_proj", 1, 0, "act", "cur", (12, 13, 15, 16)),
    ("col_sums", 0, 1, "act", "routed", (22,)),
    ("v_proj", 0, 0, "dve", "cur", (20, 21, 23, 24)),
    ("max_rows", 0, 1, "act", "cur", (25,)),
    ("out_rows", 2, 1, "dve", "prev", (28,)),
    ("v_proj", 1, 0, "dve", "cur", (29, 31, 32, 33)),
    ("col_sums", 1, 1, "act", "routed", (33,)),
    ("x_cols", 0, 1, "act", "next", (35,)),
    ("x_cols", 1, 0, "act", "next", (37,)),
    ("max_rows", 1, 1, "act", "cur", (38,)),
    ("out_rows", 3, 1, "dve", "prev", (41,)),
    ("q_proj", 0, 0, "act", "next", (40, 41, 42, 43)),
    ("col_sums", 2, 1, "act", "routed", (44,)),
    ("att_cols", 0, 1, "act", "prev", (47,)),
    ("k_proj", 0, 0, "act", "next", (46, 47, 48, 49)),
    ("att_cols", 1, 1, "act", "prev", (50,)),
    ("max_rows", 2, 1, "act", "cur", (53,)),
    ("ranks", 0, 1, "dve", "routed", (55,)),
    ("att_out", 0, 0, "dve", "prev", (54, 55, 56, 57)),
    ("out_rows", 0, 0, "dve", "cur", (60,)),
    ("att_out", 1, 1, "dve", "prev", (58, 59, 60, 61)),
]


def same_batch(arg):
    return arg < 3


def present(b, who):
    return {"cur": b < BATCHES, "prev": 0 < b <= BATCHES, "next": b < BATCHES - 1, "routed": b > 1}[who]


def bank_of(name, arg):
    return next(bank for n, a, bank, _, _, _ in MISC if (n, a) == (name, arg))


def jobs_before(b, name, arg):
    n = 0
    for other, a, bank, _, who, _ in MISC:
        if (other, a) == (name, arg):
            return n
        if bank == bank_of(name, arg) and present(b, who):
            n += 1
    raise ValueError(name)


def jobs_in(b, bank):
    return sum(1 for _, _, bk, _, who, _ in MISC if bk == bank and present(b, who))


def filled(b, name, arg):
    bank = bank_of(name, arg)
    if isinstance(b, int):
        return sum(jobs_in(i, bank) for i in range(b)) + jobs_before(b, name, arg) + 1
    ahead = jobs_in(0, bank) + jobs_in(1, bank) - 2 * jobs_in(2, bank)
    return b * jobs_in(2, bank) + (ahead + jobs_before(2, name, arg) + 1)


def build(nc, x, Wq, bq, Wk, bk, Wv, bv, Wo, router_w, router_b, temperature, wg, wp, wo, out):
    B, N, E = x.shape
    H, D = 16, E // 16
    NE, _, FF = wg.shape
    KT = E // P
    TT = N // P
    GROUPS, GH = 4, 4
    STEP = GH * TT
    UNITS = GROUPS * STEP
    QROWS = PAIRS * D
    MASK_ROW = QROWS
    MAX_ROW = QROWS + 2
    SROWS = MAX_ROW + 3
    K_LAST, K_FIRST, MINUS, Q_FIRST, Q_LAST = range(5)
    BATCH_TILES = B * TT
    SCALE = float(D) ** -0.5
    J = BATCH_TILES
    TOP = 2
    REGION = B * N + P
    MIN_TILES = TOP * B * N // P
    NT = (TOP * B * N + NE * (P - 1)) // P
    BEYOND = NT - MIN_TILES + 1
    ROW = E + 2
    ITERS = 3
    IOTAS = 8
    ROUTE_START = 13
    PERIOD = 11
    FT = FF // P
    assert out.shape[0] == B * N + P
    assert (B, TT, KT, H) == (BATCHES, 4, 2, 16) and NE * KT == B

    with ExitStack() as ctx:
        def sb(name, shape, dt):
            return ctx.enter_context(nc.sbuf_tensor(name, shape, dt))

        def psum(name, shape, dt):
            return ctx.enter_context(nc.psum_tensor(name, shape, dt))

        def sem(name):
            return ctx.enter_context(nc.semaphore(name))

        s1 = psum("s1", [P, 3, 512], F32)
        s2 = psum("s2", [P, 2, 512], F32)
        pv = psum("pv", [P, 512], F32)
        misc = psum("misc", [P, 2, 512], F32)

        stacks = sb("stacks", [P, 2, H, N], BF16)
        qst = stacks[:, 0, :, :]
        kst = stacks[:, 1, :, :]
        prob = sb("prob", [P, 2, GH, N], F32)
        vau = sb("vau", [P, TT, H, 2 * D], F32)
        xin = sb("xin", [P, TT, E], F32)
        xc = sb("xc", [P, KT, N], F32)
        qk32 = sb("qk32", [P, 2, 2, N], F32)
        rest = sb("rest", [P, N], F32)
        parts = sb("parts", [P, 2, 2, 3, N], BF16)
        o32 = sb("o32", [P, N], F32)
        att = sb("att", [P, TT, E], F32)
        attc = sb("attc", [P, KT, N], F32)
        xres = sb("xres", [P, TT, E], F32)
        srow = sb("srow", [P, TOP, TT, ROW], F32)
        xn = srow[:, 0, :, 0:E]
        xnc = sb("xnc", [P, KT, N], F32)
        rden = sb("rden", [P, TT, GH], F32)
        mx = sb("mx", [P, 2, TT, GH], F32)
        mxleft = sb("mxleft", [P, TT, GH], F32)
        mxparts = sb("mxparts", [P, 2, TT, 3, GH], BF16)
        mrows = sb("mrows", [3 * GH, N], BF16)
        stats = sb("stats", [P, 2, TT, 6], F32)
        mv = sb("mv", [P, 2, TT, 2], F32)
        rstd = sb("rstd", [P, 2, TT], F32)
        varp = sb("varp", [P, 2, TT], F32)
        nhalf = sb("nhalf", [P, TT], F32)
        ident = sb("ident", [P, P], F32)
        identb = sb("identb", [P, P], BF16)
        wqT = sb("wqT", [P, KT, E], F32)
        wkT = sb("wkT", [P, KT, E], F32)
        wvT = sb("wvT", [P, KT, E], F32)
        woT = sb("woT", [P, KT, E], F32)
        wnat = prob[:, 0, 0:4, :].rearrange("p m (f e) -> p m f e", f=2)
        bias = sb("bias", [P, 2, 2], F32)
        bvb = sb("bvb", [P, E], F32)
        rw = sb("rw", [NE, E], F32)
        rwT = sb("rwT", [P, KT, NE], F32)
        rbb = sb("rbb", [P, NE], F32)
        tmp1 = sb("tmp1", [P, 1], F32)
        tinv = sb("tinv", [P, 1], F32)
        edge = sb("edge", [1, 5, N], BF16)

        sc = sb("sc", [P, TT, NE], F32)
        ex = sb("ex", [P, TT, NE], F32)
        row_red = sb("row_red", [P, TT], F32)
        row_log = sb("row_log", [P, TT], F32)
        col_red = sb("col_red", [P, 2, NE], F32)
        col_log = sb("col_log", [P, NE], F32)
        col_sum = sb("col_sum", [P, 2, NE], F32)
        gates = sb("gates", [P, TT, NE], F32)
        match = sb("match", [P, TT, NE], F32)
        sel = sb("sel", [P, TOP, TT, NE], F32)
        chosen = sb("chosen", [P, TT + 1, NE], F32)
        topv = sb("topv", [P, TOP, TT], F32)
        slotf = sb("slotf", [P, TT, NE], F32)
        posf = sb("posf", [P, TOP, TT], F32)
        sidx = sb("sidx", [P, TOP, TT], U32)
        next_slot = sb("next_slot", [P, NE], F32)
        lower = sb("lower", [P, P], F32)
        ones = sb("ones", [P, P], F32)
        rev = sb("rev", [P, NE], F32)
        regoff = sb("regoff", [P, NE], F32)
        kk = sb("kk", [1, J], F32)
        ti = sb("ti", [1, NT], F32)
        cmp1 = o32[0:1, :].rearrange("p (e j) -> p e j", e=NE)
        free1 = parts[0:1, :, :, :, :].rearrange("p a b c n -> p (a b c n)").bitcast(F32)
        cmp2 = free1[:, 0:NT * NE].rearrange("p (t e) -> p t e", e=NE)
        cmp3 = free1[:, NT * NE:2 * NT * NE].rearrange("p (t e) -> p t e", e=NE)
        tiles = sb("tiles", [1, 2, NE], F32)
        tabf = sb("tabf", [1, 3, NT], F32)
        tabu = sb("tabu", [1, 2, NT], U32)
        count1 = sb("count1", [1, NE], F32)
        padu = sb("padu", [1, NE], U32)
        padrow = sb("padrow", [P, ROW], F32)
        wgs = sb("wgs", [P, NE * KT, FF], F32)
        wps = sb("wps", [P, NE * KT, FF], F32)
        wos = stacks[:, :, :, :].rearrange("p a h n -> p (a h n)").bitcast(F32).rearrange("p (f e) -> p f e", e=E)
        gsb, hsb = xc[:, 0, :], xc[:, 1, :]
        hT = attc[:, 0, :].rearrange("p (f n) -> p f n", f=FT)
        tinT = attc[:, 1, 0:KT * P].rearrange("p (k n) -> p k n", k=KT)
        tin, ysb = xnc[:, 0, 0:ROW], xnc[:, 1, 0:E]
        meta = sb("meta", [P, 3, 2], F32)
        yidx = sb("yidx", [P, 1], U32)

        slots_d = nc.dram_tensor("slots_scratch", (NE * REGION + BEYOND * P, ROW), F32, kind="Internal").ap()

        passed = sem("passed")
        w_loaded = sem("w_loaded")
        small_loaded = sem("small_loaded")
        const_set = sem("const_set")
        edge_set = sem("edge_set")
        edges_placed = sem("edges_placed")
        ident_set = sem("ident_set")
        w_turned = sem("w_turned")
        w_copied = sem("w_copied")
        bias_scaled = sem("bias_scaled")
        x_loaded = sem("x_loaded")
        xres_loaded = sem("xres_loaded")
        ln_stats = [sem("ln1_stats"), sem("ln2_stats")]
        ln_mean = [sem("ln1_mean"), sem("ln2_mean")]
        ln_varp = [sem("ln1_varp"), sem("ln2_varp")]
        ln_rstd = [sem("ln1_rstd"), sem("ln2_rstd")]
        ln_done = [sem("ln1_done"), sem("ln2_done")]
        s1_full, s1_read = sem("s1_full"), sem("s1_read")
        s2_full, exp_done = sem("s2_full"), sem("exp_done")
        pv_part = sem("pv_part")
        o_read = sem("o_read")
        rden_set = sem("rden_set")
        job_full = [sem("job_full0"), sem("job_full1")]
        job_read = [sem("job_read0"), sem("job_read1")]
        split_step = sem("split_step")
        q_split = sem("q_split")
        parts_set = [sem("parts_set0"), sem("parts_set1")]
        msplit_step = sem("msplit_step")
        mhigh_set = sem("mhigh_set")
        mparts_set = sem("mparts_set")
        stack_placed = [sem(f"stack_placed{g}") for g in range(GROUPS)]
        max_placed = [sem(f"max_placed{g}") for g in range(GROUPS)]
        base_set = sem("base_set")
        base_stored = sem("base_stored")
        tinv_set = sem("tinv_set")
        less_row_max, row_exp_set = sem("less_row_max"), sem("row_exp_set")
        row_sum_set, row_log_set = sem("row_sum_set"), sem("row_log_set")
        part_max_set, col_max_set = sem("part_max_set"), sem("col_max_set")
        col_log_set, col_inv_set = sem("col_log_set"), sem("col_inv_set")
        less_col_max, col_exp_set = sem("less_col_max"), sem("col_exp_set")
        balanced, gates_set = sem("balanced"), sem("gates_set")
        route_const = sem("route_const")
        iota_set = sem("iota_set")
        route_chain = sem("route_chain")
        dve_chain = sem("dve_chain")
        sel_set = sem("sel_set")
        slotf_set = sem("slotf_set")
        table_set = sem("table_set")
        pads_set = sem("pads_set")
        pad_placed = sem("pad_placed")
        beyond_placed = sem("beyond_placed")
        srow_set = sem("srow_set")
        srow_placed = [sem("srow_placed0"), sem("srow_placed1")]
        up_loaded = sem("up_loaded")
        down_loaded = sem("down_loaded")
        tin_loaded = sem("tin_loaded")
        tinT_full, tinT_read = sem("tinT_full"), sem("tinT_read")
        g_full, g_read = sem("g_full"), sem("g_read")
        p_full, h_set = sem("p_full"), sem("h_set")
        hT_full, hT_read = sem("hT_full"), sem("hT_read")
        y_full, y_read = sem("y_full"), sem("y_read")
        meta_taken = sem("meta_taken")
        meta_step = sem("meta_step")
        y_added = sem("y_added")
        y_read_meta = sem("y_read_meta")

        block = ctx.enter_context(nc.Block())

        def s1_bank(at):
            return 1 if at == UNITS - 1 else at % 3

        def is_reg(v):
            return not isinstance(v, int)

        def wait(eng, s, v):
            if is_reg(v) or v > 0:
                eng.wait_ge(s, v)

        def wait_apart(eng, s, v):
            wait(eng, s, v)
            if is_reg(v):
                eng.sem_inc(passed, 1)

        def here(b, who):
            return True if is_reg(b) else present(b, who)

        def over_batches(eng, body):
            for b in range(3):
                body(b)
            with eng.Fori(3, B - 1) as b:
                body(b)
            for b in range(B - 1, B + 2):
                body(b)

        def emptied(b, at, engine):
            return [(n, a) for n, a, _, e, who, places in MISC
                    if places[-1] + 1 == at and e == engine and here(b, who)]

        def wait_other(eng, sems, b, name, arg, bank):
            if bank_of(name, arg) != bank:
                wait(eng, sems[bank_of(name, arg)], filled(b, name, arg))

        def wait_job(eng, b, name, arg):
            wait(eng, job_full[bank_of(name, arg)], filled(b, name, arg))

        @block.tensor
        def _(pe):
            def mm(o, l, r, start=True, stop=True):
                return nc.tensor.matmul(o, l, r, start=start, stop=stop)

            pe.wait_ge(ident_set, 3)
            pe.wait_ge(w_loaded, 16 * 4)
            for m in range(4):
                for e in range(KT):
                    n = 2 * m + e
                    if n >= 2:
                        pe.wait_ge(w_copied, n - 1)
                    for f in range(2):
                        last = nc.tensor.transpose(s1[:, n % 2, f * P:(f + 1) * P],
                                                   wnat[:, m, f, e * P:(e + 1) * P], ident[:, :])
                    last.then_inc(w_turned, 1)
            pe.wait_ge(small_loaded, 16 * 12)
            pe.wait_ge(w_copied, 7)
            for e in range(KT):
                last = nc.tensor.transpose(s1[:, 0, e * NE:(e + 1) * NE], rw[:, e * P:(e + 1) * P], ident[0:NE, 0:NE])
            last.then_inc(w_turned, 1)
            pe.wait_ge(w_copied, 9)

            def job(b, name, arg, piece, pieces):
                bank = bank_of(name, arg)
                o = misc[:, bank, :]
                if piece == 0:
                    wait(pe, job_read[bank], filled(b, name, arg) - 1)
                if name == "max_rows":
                    bb = b if same_batch(arg) else b - 1
                    pe.wait_ge(mparts_set, bb * GROUPS + arg + 1)
                    rows16 = o[0:3 * GH, :].bitcast(BF16)
                    for t in range(TT):
                        last = nc.tensor.transpose(rows16[:, t * P:(t + 1) * P],
                                                   mxparts[:, arg % 2, t, :, :].rearrange("p i h -> p (i h)"), identb[:, :])
                elif name in ("q_proj", "k_proj"):
                    w = wqT if name == "q_proj" else wkT
                    bx = b if arg else b + 1
                    xb = b if arg == 0 else b - 1
                    if piece == 0 and (is_reg(b) or xb >= 0):
                        for k in range(KT):
                            wait_other(pe, job_read, xb, "x_cols", k, bank)
                    half, e = slice(piece // KT * (N // 2), (piece // KT + 1) * (N // 2)), piece % KT
                    last = mm(o[:, half], w[:, e, arg * P:(arg + 1) * P], xc[:, e, half], e == 0, e == KT - 1)
                elif name == "v_proj":
                    t = piece
                    for e in range(KT):
                        last = mm(o[:, t * P:(t + 1) * P], xc[:, e, t * P:(t + 1) * P],
                                  wvT[:, e, arg * P:(arg + 1) * P], e == 0, e == KT - 1)
                elif name == "x_cols":
                    pe.wait_ge(ln_done[0], (b + 2) * TT)
                    for t in range(TT):
                        last = nc.tensor.transpose(o[:, t * P:(t + 1) * P], xin[:, t, arg * P:(arg + 1) * P], ident[:, :])
                elif name == "out_rows":
                    bb = b if arg == 0 else b - 1
                    pe.wait_ge(o_read, bb * GROUPS + arg + 1)
                    for t in range(TT):
                        last = nc.tensor.transpose(o[:, t * P:(t + 1) * P], o32[:, t * P:(t + 1) * P], ident[:, :])
                elif name == "att_cols":
                    wait_other(pe, job_read, b, "out_rows", 3, bank)
                    for t in range(TT):
                        last = nc.tensor.transpose(o[:, t * P:(t + 1) * P], att[:, t, arg * P:(arg + 1) * P], ident[:, :])
                elif name == "att_out":
                    if piece == 0:
                        wait_other(pe, job_read, b, "att_cols", 1, bank)
                    t, k = piece // KT, piece % KT
                    last = mm(o[:, t * E:(t + 1) * E], attc[:, k, (2 * arg + t) * P:(2 * arg + t + 1) * P],
                              woT[:, k, :], k == 0, k == KT - 1)
                elif name == "xn_cols":
                    pe.wait_ge(ln_done[1], (b - 1) * TT)
                    for t in range(TT):
                        last = nc.tensor.transpose(o[:, t * P:(t + 1) * P], xn[:, t, arg * P:(arg + 1) * P], ident[:, :])
                elif name == "router":
                    if piece == 0:
                        for k in range(KT):
                            wait_other(pe, job_read, b, "xn_cols", k, bank)
                    for t in range(2 * piece, 2 * piece + 2):
                        for k in range(KT):
                            last = mm(o[:, t * NE:(t + 1) * NE], xnc[:, k, t * P:(t + 1) * P], rwT[:, k, :],
                                      k == 0, k == KT - 1)
                elif name == "col_sums":
                    if not is_reg(b) and b == 2 and arg == 0:
                        pe.wait_ge(route_const, 4)
                    pe.wait_ge(col_exp_set, (b - 2) * ITERS + arg + 1)
                    for t in range(TT):
                        last = mm(o[:, 0:NE], ones[:, :], ex[:, t, :], t == 0, t == TT - 1)
                elif name == "ranks":
                    pe.wait_ge(sel_set, b - 1)
                    mm(o[:, 0:(TT + 1) * NE], lower[:, :], chosen[:, :, :], True, False)
                    for t in range(1, TT + 1):
                        last = mm(o[:, t * NE:(TT + 1) * NE], ones[:, :], chosen[:, 0:TT + 1 - t, :], False, t == TT)
                if piece == pieces - 1:
                    last.then_inc(job_full[bank], 1)

            def score_max(b, g, s):
                n = b * UNITS + g * STEP + s
                h, t = GH * g + s // TT, s % TT
                if s == 0:
                    pe.wait_ge(stack_placed[g], (b + 1) * 16 * 2 * PAIRS)
                    if not is_reg(b) and b == 0:
                        pe.wait_ge(edges_placed, 16 * 7)
                at = g * STEP + s
                wait(pe, s1_read, n - {UNITS - 1: 2, 0: 4, 1: 2, 2: 4}.get(at, 3) + 1)
                mm(s1[:, s1_bank(at), :], qst[0:MAX_ROW, h, t * P:(t + 1) * P], kst[0:MAX_ROW, h, :]).then_inc(s1_full, 1)

            def score_keys(b, g, u):
                n = b * UNITS + g * STEP + u
                h, t = GH * g + u % GH, u // GH
                if u == 0:
                    pe.wait_ge(max_placed[g], (b + 1) * 16 * 3)
                wait(pe, exp_done, n - 1)
                mm(s2[:, u % 2, :], kst[0:SROWS, h, t * P:(t + 1) * P], qst[0:SROWS, h, :]).then_inc(s2_full, 1)

            def weigh_values(b, g, t):
                pe.wait_ge(exp_done, b * UNITS + g * STEP + GH * (t + 1))
                if t == 0:
                    wait(pe, o_read, b * GROUPS + g)
                    wait(pe, job_read[bank_of("v_proj", g // 2)], filled(b, "v_proj", g // 2))
                for j in range(GH):
                    last = mm(pv[32 * j:32 * j + 32, :], vau[:, t, GH * g + j, :], prob[:, t % 2, j, :],
                              t == 0, t == TT - 1)
                last.then_inc(pv_part, 1)

            def body(b):
                for step in range(GROUPS):
                    g2 = (step + 2) % GROUPS
                    b2 = b if step >= 2 else b - 1
                    g3 = (step + 1) % GROUPS
                    b3 = b if step >= 3 else b - 1
                    do2 = here(b, "cur" if step >= 2 else "prev")
                    do3 = here(b, "cur" if step >= 3 else "prev")
                    for s in range(STEP):
                        if here(b, "cur"):
                            score_max(b, step, s)
                        if do2:
                            score_keys(b2, g2, s)
                        if s == 2 and do3:
                            weigh_values(b3, g3, TT - 1)
                        if s in (6, 10, 14) and do2:
                            weigh_values(b2, g2, (s - 6) // 4)
                        for name, arg, _, _, who, places in MISC:
                            if STEP * step + s in places and here(b, who):
                                job(b, name, arg, places.index(STEP * step + s), len(places))

            pe.wait_ge(const_set, 2)
            for e in range(KT):
                pe.wait_ge(ln_done[0], TT)
                for t in range(TT):
                    last = nc.tensor.transpose(s1[:, e, t * P:(t + 1) * P], xin[:, t, e * P:(e + 1) * P], ident[:, :])
                last.then_inc(w_turned, 1)
            for qk in range(2):
                w = (wqT, wkT)[qk]
                pe.wait_ge(w_copied, 11)
                for e in range(KT):
                    last = mm(misc[:, qk, :], w[:, e, 0:P], xc[:, e, :], e == 0, e == KT - 1)
                last.then_inc(w_turned, 1)
            pe.wait_ge(w_copied, 13)
            over_batches(pe, body)

            tile_g, tile_p, tile_hT, tile_y, tile_t = s1[:, 0, :], s1[:, 1, :], s2[:, 0, :], s2[:, 1, 0:E], s1[:, 2, 0:KT * P]

            def turn_in(i):
                pe.wait_ge(tin_loaded, 16 * (i + 1))
                wait(pe, tinT_read, i)
                for e in range(KT):
                    last = nc.tensor.transpose(tile_t[:, e * P:(e + 1) * P], tin[:, e * P:(e + 1) * P], ident[:, :])
                last.then_inc(tinT_full, 1)

            def up(i, w, o, expert, full, read):
                pe.wait_ge(tinT_read, i + 1)
                wait(pe, read, i)
                for e in range(KT):
                    last = nc.tensor.matmul(o, tinT[:, e, :], w[:, bass.ds(expert * KT + e, 1), :],
                                            start=e == 0, stop=e == KT - 1)
                last.then_inc(full, 1)

            def turn_hidden(i):
                pe.wait_ge(h_set, i + 1)
                wait(pe, hT_read, i)
                for f in range(FT):
                    last = nc.tensor.transpose(tile_hT[:, f * P:(f + 1) * P], hsb[:, f * P:(f + 1) * P], ident[:, :])
                last.then_inc(hT_full, 1)

            def down(i, expert):
                pe.wait_ge(hT_read, i + 1)
                wait(pe, y_read, i)
                for f in range(FT):
                    last = nc.tensor.matmul(tile_y, hT[:, f, :], wos[:, bass.ds(expert * FT + f, 1), :],
                                            start=f == 0, stop=f == FT - 1)
                last.then_inc(y_full, 1)

            def tile(i, first=False, last=False):
                if not last:
                    expert = pe.value_load(tabu[0:1, 1, bass.ds(i, 1)], min_val=0, max_val=NE - 1)
                if not first:
                    before = pe.value_load(tabu[0:1, 1, bass.ds(i - 1, 1)], min_val=0, max_val=NE - 1)
                if not last:
                    up(i, wgs, tile_g, expert, g_full, g_read)
                if not first:
                    turn_hidden(i - 1)
                if not last:
                    up(i, wps, tile_p, expert, p_full, h_set)
                    if is_reg(i) or i < NT - 1:
                        turn_in(i + 1)
                if not first:
                    down(i - 1, before)

            pe.wait_ge(table_set, 1)
            pe.wait_ge(up_loaded, 16 * 2 * B)
            turn_in(0)
            tile(0, first=True)
            pe.wait_ge(down_loaded, 16)
            tile(1)
            with pe.Fori(2, NT - 1) as i:
                tile(i)
            tile(NT - 1)
            tile(NT, last=True)

        @block.scalar
        def _(act):
            def copy(o, i):
                return nc.scalar.activation(o, i, ACT.Copy)

            act.preload_act_table_set("natural_log_exp_and_others")
            for m in range(4):
                for e in range(KT):
                    n = 2 * m + e
                    act.wait_ge(w_turned, n + 1)
                    dst = (wqT, wkT, wvT, woT)[m][:, e, :]
                    src = s1[:, n % 2, 0:E]
                    if m < 2:
                        for q in range(4):
                            last = copy(dst[:, q * 64:(q + 1) * 64].rearrange("p (d h) -> p h d", h=GH),
                                        src[:, q * 64:(q + 1) * 64].rearrange("p (h d) -> p h d", h=GH))
                    else:
                        last = copy(dst, src)
                    last.then_inc(w_copied, 1)
            act.wait_ge(w_turned, 9)
            copy(rwT[:, :, :], s1[:, 0, 0:KT * NE].rearrange("p (k n) -> p k n", k=KT)).then_inc(w_copied, 1)
            act.wait_ge(small_loaded, 16 * 12)
            act.mul(bias[:, :, 0], bias[:, :, 0], SCALE).then_inc(bias_scaled, 1)
            act.wait_ge(bias_scaled, 1)
            for e in range(KT):
                act.wait_ge(w_turned, 10 + e)
                copy(xc[:, e, :], s1[:, e, :]).then_inc(w_copied, 1)

            def project_out(qk, m, src, dst):
                scale = SCALE if qk == 0 else 1.0
                return nc.scalar.activation(dst, src, ACT.Identity, bias=bias[:, m, qk:qk + 1], scale=scale)

            for qk in range(2):
                act.wait_ge(w_turned, 12 + qk)
                project_out(qk, 0, misc[:, qk, :], qk32[:, qk, 0, :])
                project_out(qk, 0, misc[:, qk, :], parts[:, 0, qk, 0, :]).then_inc(w_copied, 1)

            def job(b, name, arg):
                bank = bank_of(name, arg)
                src = misc[:, bank, :]
                wait_job(act, b, name, arg)
                if name == "max_rows":
                    bb = b if same_batch(arg) else b - 1
                    pg, pb = (arg - 1) % GROUPS, (bb if arg else bb - 1)
                    wait(act, max_placed[pg], (pb + 1) * 16 * 3)
                    last = copy(mrows[:, :], src[0:3 * GH, :].bitcast(BF16)[:, 0:N])
                elif name in ("q_proj", "k_proj"):
                    qk = 0 if name == "q_proj" else 1
                    n = b if arg else b + 1
                    wait(act, parts_set[arg], 2 * n)
                    project_out(qk, arg, src, qk32[:, qk, arg, :])
                    for g in (2 * arg, 2 * arg + 1):
                        wait(act, stack_placed[g], n * 16 * 2 * PAIRS)
                    last = project_out(qk, arg, src, parts[:, arg, qk, 0, :])
                elif name == "x_cols":
                    last_use = ("v_proj", 1)
                    wait_other(act, job_full, b, *last_use, bank)
                    last = copy(xc[:, arg, :], src)
                elif name == "att_cols":
                    if is_reg(b) or b > 1:
                        wait_other(act, job_full, b - 1, "att_out", 1, bank)
                    last = copy(attc[:, arg, :], src)
                elif name == "xn_cols":
                    if is_reg(b) or b > 2:
                        wait_other(act, job_full, b - 1, "router", 0, bank)
                    last = copy(xnc[:, arg, :], src)
                elif name == "col_sums":
                    last = nc.scalar.activation(col_log[:, :], src[:, 0:NE], ACT.Ln)
                    if arg == ITERS - 1:
                        last.then_inc(col_log_set, 1)
                        last = copy(col_sum[:, 0, :], src[:, 0:NE])
                last.then_inc(job_read[bank], 1)

            def exps(b, g, u):
                n = b * UNITS + g * STEP + u
                t = u // GH
                act.wait_ge(s2_full, n + 1)
                if u % GH == 0:
                    wait(act, pv_part, (b * GROUPS + g) * TT + t - 1)
                nc.scalar.activation(prob[:, t % 2, u % GH, :], s2[:, u % 2, :], ACT.Exp).then_inc(exp_done, 1)

            def outputs(b, g):
                n = b * GROUPS + g
                act.wait_ge(pv_part, (n + 1) * TT)
                pg = (g - 1) % GROUPS
                pb = b if g else b - 1
                it = pb + 1 if pg else pb
                if is_reg(n) or n > 0:
                    wait(act, job_full[bank_of("out_rows", pg)], filled(it, "out_rows", pg))
                copy(o32[:, :], pv[:, :]).then_inc(o_read, 1)

            def route(n, at):
                at -= ROUTE_START
                it = at // PERIOD
                if 0 <= it < ITERS:
                    if at % PERIOD == 1:
                        act.wait_ge(less_row_max, n * ITERS + it + 1)
                        nc.scalar.activation(ex[:, :, :], sc[:, :, :], ACT.Exp).then_inc(row_exp_set, 1)
                    if at % PERIOD == 3:
                        act.wait_ge(row_sum_set, n * ITERS + it + 1)
                        nc.scalar.activation(row_log[:, :], row_red[:, :], ACT.Ln).then_inc(row_log_set, 1)
                    if at % PERIOD == 7:
                        act.wait_ge(less_col_max, n * ITERS + it + 1)
                        nc.scalar.activation(ex[:, :, :], sc[:, :, :], ACT.Exp).then_inc(col_exp_set, 1)
                elif at == PERIOD * ITERS:
                    act.wait_ge(col_log_set, n + 1)
                    nc.scalar.activation(col_sum[:, 1, :], col_log[:, :], ACT.Exp, scale=-1.0).then_inc(col_inv_set, 1)
                elif at == PERIOD * ITERS + 2:
                    act.wait_ge(balanced, n + 1)
                    nc.scalar.activation(gates[:, :, :], sc[:, :, :], ACT.Exp).then_inc(gates_set, 1)

            def body(b):
                for step in range(GROUPS):
                    g2 = (step + 2) % GROUPS
                    b2 = b if step >= 2 else b - 1
                    g3 = (step + 1) % GROUPS
                    b3 = b if step >= 3 else b - 1
                    for s in range(STEP):
                        if here(b, "cur" if step >= 2 else "prev"):
                            exps(b2, g2, s)
                        if s == 3 and here(b, "cur" if step >= 3 else "prev"):
                            outputs(b3, g3)
                        if here(b, "routed"):
                            route(b - 2, STEP * step + s)
                        for name, arg in emptied(b, STEP * step + s, "act"):
                            job(b, name, arg)

            over_batches(act, body)

            def tile(i, first=False, last=False):
                if not last:
                    act.wait_ge(g_full, i + 1)
                    wait(act, h_set, i)
                    nc.scalar.activation(gsb[:, :], s1[:, 0, :], ACT.Relu).then_inc(g_read, 1)
                if not first:
                    act.wait_ge(hT_full, i)
                    wait(act, y_full, i - 1)
                    copy(hT[:, :, :], s2[:, 0, :].rearrange("p (f n) -> p f n", f=FT)).then_inc(hT_read, 1)

            tile(0, first=True)
            tile(1)
            with act.Fori(2, NT) as i:
                tile(i)
            tile(NT, last=True)

        @block.vector
        def _(dve):
            nc.vector.memset(vau[:, :, :, D:2 * D], 1.0).then_inc(const_set, 1)
            nc.vector.memset(nhalf[:, :], -0.5).then_inc(const_set, 1)

            tt, ts, red = nc.vector.tensor_tensor, nc.vector.tensor_scalar, nc.vector.tensor_reduce

            def along(a):
                return a.unsqueeze(2).broadcast_to([P, TT, NE])

            def per_expert(a):
                return a.unsqueeze(1).broadcast_to([P, TT, NE])

            def ln_statistics(which, src, b, tiles):
                if 0 in tiles:
                    wait(dve, ln_done[which], b * TT)
                for t in tiles:
                    nc.vector.bn_stats(stats[:, which, t, :], src[:, t, :]).then_inc(ln_stats[which], 1)

            def ln_means(which, b):
                for t in range(TT):
                    wait_apart(dve, ln_stats[which], b * TT + t + 1)
                    nc.vector.bn_aggr(mv[:, which, t, :], stats[:, which, t, :]).then_inc(ln_mean[which], 1)

            def ln_apply(which, dst, src, b, tiles):
                dve.wait_ge(ln_rstd[which], b + 1)
                for t in tiles:
                    nc.vector.tensor_scalar(dst[:, t, :], src[:, t, :], mv[:, which, t, 0:1], rstd[:, which, t:t + 1],
                                            ALU.subtract, ALU.mult).then_inc(ln_done[which], 1)

            def job(b, name, arg):
                bank = bank_of(name, arg)
                src = misc[:, bank, :]
                wait_job(dve, b, name, arg)
                if name == "v_proj":
                    wait(dve, pv_part, ((b - 1) * GROUPS + 2 * arg + 2) * TT)
                    last = nc.vector.tensor_tensor(
                        vau[:, :, 8 * arg:8 * arg + 8, 0:D],
                        src.rearrange("p (t h d) -> p t h d", t=TT, h=8),
                        bvb[:, arg * P:(arg + 1) * P].rearrange("p (h d) -> p h d", h=8).unsqueeze(1)
                        .broadcast_to([P, TT, 8, D]), ALU.add)
                elif name == "out_rows":
                    bb = b if arg == 0 else b - 1
                    rows = src.rearrange("p (t h d) -> p t h d", t=TT, h=GH)
                    pa, it = (arg - 1) % GROUPS, (b - 1 if arg == 1 else b)
                    if is_reg(b) or b > 1 or (arg, b) not in ((0, 0),):
                        wait(dve, job_read[bank_of("out_rows", pa)], filled(it, "out_rows", pa))
                    nc.vector.reciprocal(rden[:, :, :], rows[:, :, :, D]).then_inc(rden_set, 1)
                    dve.wait_ge(rden_set, bb * GROUPS + arg + 1)
                    if arg == 0 and (is_reg(bb) or bb > 0):
                        wait_other(dve, job_full, b, "att_cols", 1, bank)
                    last = nc.vector.tensor_tensor(
                        att[:, :, arg * GH * D:(arg + 1) * GH * D].rearrange("p t (h d) -> p t h d", h=GH),
                        rows[:, :, :, 0:D],
                        rden[:, :, :].unsqueeze(3).broadcast_to([P, TT, GH, D]), ALU.mult)
                elif name == "att_out":
                    if arg == 0:
                        dve.wait_ge(xres_loaded, 16 * b)
                    last = nc.vector.tensor_tensor(xres[:, 2 * arg:2 * arg + 2, :],
                                                   src.rearrange("p (t e) -> p t e", t=2),
                                                   xres[:, 2 * arg:2 * arg + 2, :], ALU.add)
                elif name == "router":
                    last = tt(sc[:, :, :], src[:, 0:TT * NE].rearrange("p (t n) -> p t n", t=TT), per_expert(rbb[:, :]),
                              ALU.add)
                elif name == "ranks":
                    tt(slotf[:, :, :], src[:, 0:TT * NE].rearrange("p (t n) -> p t n", t=TT),
                       per_expert(next_slot[:, :]), ALU.add).then_inc(slotf_set, 1)
                    dve.wait_ge(slotf_set, b - 1)
                    last = tt(next_slot[:, :], next_slot[:, :], src[:, TT * NE:(TT + 1) * NE], ALU.add)
                last.then_inc(job_read[bank], 1)

            routed = [0]
            ROUTE_LINKS = 31

            def route(n, at):
                def link(ins):
                    routed[0] += 1
                    ins.then_inc(route_chain, 1)
                    dve.wait_ge(route_chain, n * ROUTE_LINKS + routed[0])

                at -= ROUTE_START
                if at == 0:
                    routed[0] = 0
                    wait(dve, job_read[bank_of("router", 0)], filled(n + 2, "router", 0))
                    link(ts(sc[:, :, :], sc[:, :, :], tinv[:, 0:1], None, ALU.mult))
                it = at // PERIOD
                if at % PERIOD == 0 and 0 < it < ITERS:
                    wait(dve, job_read[bank_of("col_sums", it - 1)], filled(n + 2, "col_sums", it - 1))
                    link(tt(sc[:, :, :], sc[:, :, :], per_expert(col_log[:, :]), ALU.subtract))
                if at == PERIOD * ITERS + 1:
                    wait(dve, job_read[bank_of("col_sums", ITERS - 1)], filled(n + 2, "col_sums", ITERS - 1))
                    dve.wait_ge(col_inv_set, n + 1)
                    link(tt(col_sum[:, 1, :], col_sum[:, 0, :], col_sum[:, 1, :], ALU.mult))
                    link(nc.vector.scalar_tensor_tensor(out=col_log[:, :], in0=col_sum[:, 1, :], scalar=-1.0,
                                                        in1=col_log[:, :], op0=ALU.add, op1=ALU.add))
                    tt(sc[:, :, :], sc[:, :, :], per_expert(col_log[:, :]), ALU.subtract).then_inc(balanced, 1)
                if 0 <= it < ITERS:
                    done = n * ITERS + it + 1
                    if at % PERIOD == 0:
                        link(red(row_red[:, :], sc[:, :, :], AX_X, ALU.max))
                        tt(sc[:, :, :], sc[:, :, :], along(row_red[:, :]), ALU.subtract).then_inc(less_row_max, 1)
                    if at % PERIOD == 2:
                        dve.wait_ge(row_exp_set, done)
                        red(row_red[:, :], ex[:, :, :], AX_X, ALU.add).then_inc(row_sum_set, 1)
                    if at % PERIOD == 4:
                        dve.wait_ge(row_log_set, done)
                        link(tt(sc[:, :, :], sc[:, :, :], along(row_log[:, :]), ALU.subtract))
                        red(col_red[:, 0, :], sc[:, :, :].rearrange("p t e -> p e t"), AX_X, ALU.max)\
                            .then_inc(part_max_set, 1)
                    if at % PERIOD == 6:
                        dve.wait_ge(col_max_set, done)
                        tt(sc[:, :, :], sc[:, :, :], per_expert(col_red[:, 1, :]), ALU.subtract).then_inc(less_col_max, 1)
                if at == 18:
                    wait(dve, srow_placed[1], 16 * TT * n)
                    nc.vector.tensor_copy(srow[:, 1, :, 0:E], srow[:, 0, :, 0:E]).then_inc(srow_set, 1)
                if at == 36:
                    dve.wait_ge(gates_set, n + 1)
                    link(red(row_red[:, :], gates[:, :, :], AX_X, ALU.add))
                    link(ts(row_red[:, :], row_red[:, :], 1e-8, None, ALU.add))
                    link(nc.vector.reciprocal(row_red[:, :], row_red[:, :]))
                    link(tt(gates[:, :, :], gates[:, :, :], along(row_red[:, :]), ALU.mult))
                if at in (37, 39):
                    c = (at - 37) // 2
                    if c:
                        link(nc.vector.scalar_tensor_tensor(out=gates[:, :, :], in0=sel[:, 0, :, :], scalar=-4.0,
                                                            in1=gates[:, :, :], op0=ALU.mult, op1=ALU.add))
                    link(red(topv[:, c, :], gates[:, :, :], AX_X, ALU.max))
                    link(tt(match[:, :, :], gates[:, :, :], along(topv[:, c, :]), ALU.is_equal))
                if at in (38, 40):
                    c = (at - 38) // 2
                    link(tt(match[:, :, :], match[:, :, :], per_expert(rev[:, :]), ALU.mult))
                    link(red(row_red[:, :], match[:, :, :], AX_X, ALU.max))
                    link(tt(sel[:, c, :, :], along(row_red[:, :]), per_expert(rev[:, :]), ALU.is_equal))
                if at == 40:
                    tt(chosen[:, 0:TT, :], sel[:, 0, :, :], sel[:, 1, :, :], ALU.add).then_inc(sel_set, 1)
                if at == 41:
                    link(tt(row_red[:, :], topv[:, 0, :], topv[:, 1, :], ALU.add))
                    link(ts(row_red[:, :], row_red[:, :], 1e-8, None, ALU.add))
                    link(nc.vector.reciprocal(row_red[:, :], row_red[:, :]))
                    tt(srow[:, :, :, E + 1], topv[:, :, :], row_red[:, :].unsqueeze(1).broadcast_to([P, TOP, TT]),
                       ALU.mult).then_inc(srow_set, 1)
                    ts(srow[:, :, :, E], srow[:, :, :, E], float(N), None, ALU.add).then_inc(srow_set, 1)
                if at == 44:
                    dve.wait_ge(slotf_set, n + 1)
                    link(tt(sel[:, :, :, :], sel[:, :, :, :],
                            slotf[:, :, :].unsqueeze(1).broadcast_to([P, TOP, TT, NE]), ALU.mult))
                    link(red(posf[:, :, :], sel[:, :, :, :], AX_X, ALU.add))
                    nc.vector.tensor_copy(sidx[:, :, :], posf[:, :, :]).then_inc(srow_set, 1)
                    assert routed[0] == ROUTE_LINKS

            def maxima(b, g, s):
                n = b * UNITS + g * STEP + s
                if s == 0:
                    wait(dve, mparts_set, b * GROUPS + g - 1)
                dve.wait_ge(s1_full, n + 1)
                nc.vector.tensor_reduce(mx[:, g % 2, s % TT, s // TT:s // TT + 1], s1[:, s1_bank(g * STEP + s), :], AX_X, ALU.max)\
                    .then_inc(s1_read, 1)

            def body(b):
                for step in range(GROUPS):
                    for s in range(STEP):
                        if here(b, "cur"):
                            maxima(b, step, s)
                        at = (step, s)
                        if here(b, "next"):
                            if at == (0, 5):
                                dve.wait_ge(x_loaded, 16 * (b + 2))
                            if at in ((0, 5), (0, 7)):
                                ln_statistics(0, xin, b + 1, ((0, 1) if s == 5 else (2, 3)))
                            if at == (0, 9):
                                ln_means(0, b + 1)
                            if at in ((1, 2), (1, 5)):
                                ln_apply(0, xin, xin, b + 1, ((0, 1) if s == 2 else (2, 3)))
                        if here(b, "prev"):
                            if at in ((3, 11), (3, 15)):
                                i = (s - 11) // 4
                                wait(dve, job_read[bank_of("att_out", i)], filled(b, "att_out", i))
                                ln_statistics(1, xres, b - 1, (2 * i, 2 * i + 1))
                        if here(b, "routed"):
                            if at == (0, 0):
                                ln_means(1, b - 2)
                            if at == (0, 2):
                                if is_reg(b) or b > 2:
                                    dve.wait_ge(srow_placed[0], 16 * TT * (b - 2))
                                    dve.wait_ge(base_set, b - 2)
                                    wait(dve, job_full[bank_of("xn_cols", 1)], filled(b - 1, "xn_cols", 1))
                                ln_apply(1, xn, xres, b - 2, range(TT))
                        if here(b, "routed"):
                            route(b - 2, STEP * step + s)
                        for name, arg in emptied(b, STEP * step + s, "dve"):
                            job(b, name, arg)

            dve.wait_ge(x_loaded, 16)
            ln_statistics(0, xin, 0, range(TT))
            ln_means(0, 0)
            ln_apply(0, xin, xin, 0, range(TT))
            dve.wait_ge(w_copied, 12)
            left = att[:, 0:2, :].rearrange("p t e -> p (t e)")
            hi, mid, lo = (parts[:, 0, 0, i, :] for i in range(3))
            tt(left, qk32[:, 0, 0, :], hi, ALU.subtract).then_inc(q_split, 1)
            dve.wait_ge(q_split, 1)
            nc.vector.tensor_copy(mid, left).then_inc(q_split, 1)
            dve.wait_ge(q_split, 2)
            tt(lo, left, mid, ALU.subtract).then_inc(q_split, 1)
            dve.wait_ge(small_loaded, 16 * 12)
            ts(tinv[:, :], tmp1[:, :], 0.1, None, ALU.max).then_inc(tinv_set, 1)
            dve.wait_ge(tinv_set, 1)
            nc.vector.reciprocal(tinv[:, :], tinv[:, :]).then_inc(tinv_set, 1)
            dve.wait_ge(tinv_set, 2)
            dve.wait_ge(iota_set, IOTAS)
            over_batches(dve, body)

            count = [0]

            def link(ins):
                count[0] += 1
                ins.then_inc(dve_chain, 1)
                dve.wait_ge(dve_chain, count[0])

            wait(dve, job_read[bank_of("ranks", 0)], filled(B + 1, "ranks", 0))
            nc.vector.tensor_copy(padu[:, :], next_slot[0:1, :]).then_inc(pads_set, 1)
            n_e = count1[:, :]
            link(tt(n_e, next_slot[0:1, :], regoff[0:1, :], ALU.subtract))
            link(tt(cmp1, n_e.unsqueeze(2).broadcast_to([1, NE, J]), kk[:, :].unsqueeze(1).broadcast_to([1, NE, J]),
                    ALU.is_gt))
            link(red(tiles[:, 0, :], cmp1, AX_X, ALU.add))
            link(nc.vector.tensor_tensor_scan(tiles[:, 1, :], ones[0:1, 0:NE], tiles[:, 0, :], 0.0, ALU.mult, ALU.add))
            over_e = [1, NT, NE]
            link(tt(cmp2, ti[:, :].unsqueeze(2).broadcast_to(over_e), tiles[:, 1, :].unsqueeze(1).broadcast_to(over_e),
                    ALU.is_ge))
            link(tt(cmp3, cmp2, tiles[:, 0, :].unsqueeze(1).broadcast_to(over_e), ALU.mult))
            link(red(tabf[:, 0, :], cmp2, AX_X, ALU.add))
            link(red(tabf[:, 1, :], cmp3, AX_X, ALU.add))
            link(tt(tabf[:, 1, :], ti[:, :], tabf[:, 1, :], ALU.subtract))
            link(ts(tabf[:, 1, :], tabf[:, 1, :], float(P), None, ALU.mult))
            link(ts(tabf[:, 2, :], tabf[:, 0, :], float(REGION), None, ALU.mult))
            link(tt(tabf[:, 1, :], tabf[:, 1, :], tabf[:, 2, :], ALU.add))
            link(ts(tabf[:, 0, :], tabf[:, 0, :], float(NE - 1), None, ALU.min))
            link(nc.vector.tensor_copy(tabu[:, 1, :], tabf[:, 0, :]))
            nc.vector.tensor_copy(tabu[:, 0, :], tabf[:, 1, :]).then_inc(table_set, 1)
            def turn_out(i):
                dve.wait_ge(tinT_full, i + 1)
                nc.vector.tensor_copy(meta[:, 0, :], tin[:, E:E + 2]).then_inc(meta_taken, 1)
                nc.vector.tensor_copy(tinT[:, :, :], s1[:, 2, 0:KT * P].rearrange("p (k n) -> p k n", k=KT))\
                    .then_inc(tinT_read, 1)

            def tile(i, first=False, last=False):
                if not last:
                    dve.wait_ge(p_full, i + 1)
                    dve.wait_ge(g_read, i + 1)
                    wait(dve, hT_full, i)
                    tt(hsb[:, :], gsb[:, :], s1[:, 1, :], ALU.mult).then_inc(h_set, 1)
                    if is_reg(i) or i < NT - 1:
                        turn_out(i + 1)
                if not first:
                    dve.wait_ge(y_full, i)
                    wait(dve, y_added, 16 * (i - 1))
                    nc.vector.tensor_copy(yidx[:, :], meta[:, 2, 0:1]).then_inc(y_read_meta, 1)
                    ts(ysb[:, :], s2[:, 1, 0:E], meta[:, 2, 1:2], None, ALU.mult).then_inc(y_read, 1)
                    dve.wait_ge(y_read, i)
                if not last:
                    nc.vector.tensor_copy(meta[:, 2, :], meta[:, 1, :]).then_inc(meta_step, 1)
                    dve.wait_ge(meta_step, 2 * i + 2)
                    if is_reg(i) or i < NT - 1:
                        dve.wait_ge(meta_taken, i + 2)
                        nc.vector.tensor_copy(meta[:, 1, :], meta[:, 0, :]).then_inc(meta_step, 1)
                        dve.wait_ge(meta_step, 2 * i + 3)

            turn_out(0)
            dve.wait_ge(meta_taken, 1)
            nc.vector.tensor_copy(meta[:, 1, :], meta[:, 0, :]).then_inc(meta_step, 1)
            dve.wait_ge(meta_step, 1)
            tile(0, first=True)
            tile(1)
            with dve.Fori(2, NT - 1) as i:
                tile(i)
            tile(NT - 1)
            tile(NT, last=True)

        @block.gpsimd
        def _(pool):
            nc.gpsimd.memset(ident[:, :], 0.0).then_inc(ident_set, 1)
            pool.wait_ge(ident_set, 1)
            nc.gpsimd.affine_select(out=ident[:, :], in_=ident[:, :], compare_op=ALU.not_equal, fill=1.0, base=0,
                                    pattern=[[-1, P]], channel_multiplier=1).then_inc(ident_set, 1)
            pool.wait_ge(ident_set, 2)
            nc.gpsimd.tensor_copy(identb[:, :], ident[:, :]).then_inc(ident_set, 1)
            nc.gpsimd.memset(edge[:, :, :], 0.0).then_inc(edge_set, 1)
            pool.wait_ge(edge_set, 1)
            nc.gpsimd.memset(edge[:, K_LAST, N - 1:N], 1.0).then_inc(edge_set, 1)
            nc.gpsimd.memset(edge[:, K_FIRST, 0:1], 1.0).then_inc(edge_set, 1)
            nc.gpsimd.memset(edge[:, MINUS, :], -1.0).then_inc(edge_set, 1)
            nc.gpsimd.memset(edge[:, Q_FIRST, 0:1], NEG).then_inc(edge_set, 1)
            nc.gpsimd.memset(edge[:, Q_LAST, N - 1:N], NEG).then_inc(edge_set, 1)

            def rsqrt(which, b):
                wait_apart(pool, ln_mean[which], TT * (b + 1))
                nc.gpsimd.tensor_scalar(varp[:, which, :], mv[:, which, :, 1], LN_EPS, None, ALU.add)\
                    .then_inc(ln_varp[which], 1)
                wait_apart(pool, ln_varp[which], b + 1)
                nc.gpsimd.tensor_tensor(rstd[:, which, :], varp[:, which, :], nhalf[:, :], ALU.pow)\
                    .then_inc(ln_rstd[which], 1)

            def split_rest(value, hi, mid, lo, left, step_sem, done, n):
                nc.gpsimd.tensor_tensor(left, value, hi, ALU.subtract).then_inc(step_sem, 1)
                wait_apart(pool, step_sem, 2 * n + 1)
                nc.gpsimd.tensor_copy(mid, left).then_inc(step_sem, 1)
                wait_apart(pool, step_sem, 2 * n + 2)
                nc.gpsimd.tensor_tensor(lo, left, mid, ALU.subtract).then_inc(done, 1)

            def split_qk(b, m, qk):
                n = 4 * b + 2 * m + qk
                if is_reg(n) or n > 0:
                    if qk == 1:
                        wait_apart(pool, parts_set[m], 2 * b + 1)
                    elif m == 1:
                        wait_apart(pool, parts_set[0], 2 * b + 2)
                    else:
                        wait_apart(pool, parts_set[1], 2 * b)
                hi, mid, lo = (parts[:, m, qk, i, :] for i in range(3))
                split_rest(qk32[:, qk, m, :], hi, mid, lo, rest[:, :], split_step, parts_set[m], n)

            def split_max(b, g):
                n = GROUPS * b + g
                value = mx[:, g % 2, :, :]
                hi, mid, lo = (mxparts[:, g % 2, :, i, :] for i in range(3))
                if is_reg(n) or n > 1:
                    pg, it = {0: (2, b - 1), 1: (3, b), 2: (0, b), 3: (1, b)}[g]
                    wait_apart(pool, job_full[bank_of("max_rows", pg)], filled(it, "max_rows", pg))
                wait_apart(pool, mparts_set, n)
                wait_apart(pool, s1_read, b * UNITS + STEP * (g + 1))
                nc.gpsimd.tensor_copy(hi, value).then_inc(mhigh_set, 1)
                wait_apart(pool, mhigh_set, n + 1)
                split_rest(value, hi, mid, lo, mxleft[:, :, :], msplit_step, mparts_set, n)

            pool.wait_ge(const_set, 2)
            rsqrt(0, 0)
            pool.wait_ge(w_copied, 13)
            pool.wait_ge(q_split, 3)
            pool.sem_inc(split_step, 2)
            pool.sem_inc(parts_set[0], 1)
            split_qk(0, 0, 1)

            def scatter(n, c):
                if c == 0 or not is_reg(n):
                    wait_apart(pool, srow_set, 4 * (n + 1))
                for t in range(TT):
                    nc.gpsimd.indirect_dma_start(slots_d, bass.IndirectOffsetOnAxis(ap=sidx[:, c, t:t + 1], axis=0),
                                                 srow[:, c, t, :], None).then_inc(srow_placed[c], 16)

            def body(b):
                for at in range(GROUPS * STEP):
                    if at == 0 and here(b, "prev"):
                        split_max(b - 1, 3)
                    if at == 1 and here(b, "routed"):
                        rsqrt(1, b - 2)
                    if at == 4 and here(b, "routed"):
                        wait_apart(pool, ln_done[1], TT * (b - 1))
                        nc.gpsimd.tensor_tensor(xres[:, :, :], xres[:, :, :], xn[:, :, :], ALU.add).then_inc(base_set, 1)
                    if at in (6, 19) and here(b, "cur"):
                        qk, name = ((0, "q_proj"), (1, "k_proj"))[(at - 6) // 13]
                        wait_apart(pool, job_read[bank_of(name, 1)], filled(b, name, 1))
                        split_qk(b, 1, qk)
                    if at == 13 and here(b, "next"):
                        rsqrt(0, b + 1)
                    if at in (18, 29, 40) and here(b, "routed"):
                        it = (at - ROUTE_START) // PERIOD
                        wait_apart(pool, part_max_set, (b - 2) * ITERS + it + 1)
                        nc.gpsimd.partition_all_reduce(col_red[:, 1, :], col_red[:, 0, :], P, bass.bass_isa.ReduceOp.max)\
                            .then_inc(col_max_set, 1)
                    if at in (22, 33, 49) and here(b, "cur"):
                        split_max(b, at // STEP - 1)
                    if at in (46, 51) and here(b, "next"):
                        qk, name = ((0, "q_proj"), (1, "k_proj"))[(at - 46) // 5]
                        wait_apart(pool, job_read[bank_of(name, 0)], filled(b, name, 0))
                        split_qk(b + 1, 0, qk)
                    if at == 57 and here(b, "routed"):
                        scatter(b - 2, 0)
                    if at == 14 and (is_reg(b) or b > 2):
                        scatter(b - 3, 1)

            nc.gpsimd.memset(ones[:, :], 1.0).then_inc(route_const, 1)
            nc.gpsimd.memset(padrow[:, :], 0.0).then_inc(route_const, 1)
            pool.wait_ge(route_const, 2)
            nc.gpsimd.affine_select(out=lower[:, :], in_=ones[:, :], compare_op=ALU.is_gt, fill=0.0, base=0,
                                    pattern=[[1, P]], channel_multiplier=-1).then_inc(route_const, 1)
            nc.gpsimd.memset(chosen[:, :, :], 0.0).then_inc(route_const, 1)
            for o, pattern, base, mult in (
                    (srow[:, 0, :, E], [[P, TT]], -N, 1), (srow[:, 1, :, E], [[P, TT]], -N, 1),
                    (next_slot[:, :], [[REGION, NE]], 0, 0), (rev[:, :], [[-1, NE]], NE, 0),
                    (regoff[:, :], [[REGION, NE]], 0, 0), (kk[:, :], [[P, J]], 0, 0), (ti[:, :], [[1, NT]], 0, 0),
                    (padrow[:, E:E + 1], [[1, 1]], B * N, 1)):
                nc.gpsimd.iota(o, pattern=pattern, base=base, channel_multiplier=mult,
                                  allow_small_or_imprecise_dtypes=True).then_inc(iota_set, 1)

            over_batches(pool, body)

            scatter(B - 1, 1)

            def add(i):
                wait_apart(pool, y_read, i + 1)
                wait_apart(pool, y_read_meta, i + 1)
                wait_apart(pool, y_added, 16 * i)
                nc.gpsimd.indirect_dma_start(out, bass.IndirectOffsetOnAxis(ap=yidx[:, :], axis=0), ysb[:, :], None,
                                             compute_op=ALU.add).then_inc(y_added, 16)

            pool.wait_ge(base_stored, 16 * (B + 1))
            add(0)
            with pool.Fori(1, NT) as i:
                add(i)
            pool.wait_ge(y_added, 16 * NT)

        @block.sync
        def _(sp):
            def rows(t, b):
                return t[bass.ds(b * N, N), :].rearrange("(t p) e -> p t e", p=P)

            x_flat = x.rearrange("b n e -> (b n) e")
            sp.dma_start(xin[:, :, :], rows(x_flat, 0)).then_inc(x_loaded, 16)
            for m, w in enumerate((Wq, Wk, Wv, Wo)):
                sp.dma_start(wnat[:, m, :, :], w.rearrange("(f p) e -> p f e", p=P)).then_inc(w_loaded, 16)
            for qk, bb in enumerate((bq, bk)):
                for q in range(4):
                    src = bb[q * 64:(q + 1) * 64].rearrange("(h d o) -> d h o", h=GH, o=1)
                    with nc.allow_non_contiguous_dma("64 single biases"):
                        sp.dma_start(bias[64 * (q % 2):64 * (q % 2) + 64, q // 2, qk:qk + 1], src)\
                            .then_inc(small_loaded, 16)
            sp.dma_start(rw[:, :], router_w).then_inc(small_loaded, 16)
            with nc.allow_non_contiguous_dma("rows for all partitions"):
                sp.dma_start(bvb[:, :], bv.unsqueeze(0).broadcast_to([P, E])).then_inc(small_loaded, 16)
                sp.dma_start(rbb[:, :], router_b.unsqueeze(0).broadcast_to([P, NE])).then_inc(small_loaded, 16)
                sp.dma_start(tmp1[:, :], temperature.unsqueeze(0).broadcast_to([P, 1])).then_inc(small_loaded, 16)
            sp.wait_ge(edge_set, 6)
            for dst, row, src in ((kst, MASK_ROW, K_LAST), (kst, MASK_ROW + 1, K_FIRST), (kst, MAX_ROW, MINUS),
                                  (kst, MAX_ROW + 1, MINUS), (kst, MAX_ROW + 2, MINUS),
                                  (qst, MASK_ROW, Q_FIRST), (qst, MASK_ROW + 1, Q_LAST)):
                sp.dma_start(dst[row:row + 1, :, :], edge[:, src, :].unsqueeze(1).broadcast_to([1, H, N]))\
                    .then_inc(edges_placed, 16)

            def place_stack(b, g, which=(0, 1)):
                m, half = g // 2, g % 2
                wait_apart(sp, s2_full, (b - 1) * UNITS + (g + 1) * STEP)
                for qk in which:
                    dst, pick = ((qst, Q_PART), (kst, K_PART))[qk]
                    wait_apart(sp, parts_set[m], 2 * b + 1 + qk)
                    for c in range(PAIRS):
                        sp.dma_start(dst[c * D:(c + 1) * D, GH * g:GH * (g + 1), :],
                                     parts[64 * half:64 * half + 64, m, qk, pick[c], :]).then_inc(stack_placed[g], 16)

            def place_max(b, g):
                it = b + 1 if g == 3 else b
                wait_apart(sp, job_read[bank_of("max_rows", g)], filled(it, "max_rows", g))
                for i in range(3):
                    sp.dma_start(qst[MAX_ROW + i:MAX_ROW + i + 1, GH * g:GH * (g + 1), :],
                                 mrows[GH * i:GH * (i + 1), :]).then_inc(max_placed[g], 16)

            def body(b):
                if here(b, "next"):
                    if is_reg(b) or b > 0:
                        wait_apart(sp, job_full[bank_of("x_cols", 1)], filled(b - 1, "x_cols", 1))
                    else:
                        sp.wait_ge(w_turned, 11)
                    sp.dma_start(xin[:, :, :], rows(x_flat, b + 1)).then_inc(x_loaded, 16)
                if here(b, "cur"):
                    place_stack(b, 1)
                if here(b, "prev"):
                    place_max(b - 1, 3)
                if here(b, "routed"):
                    wait_apart(sp, base_set, b - 1)
                    sp.dma_start(rows(out, b - 2), xres[:, :, :]).then_inc(base_stored, 16)
                if here(b, "cur"):
                    place_stack(b, 2)
                    place_max(b, 0)
                if here(b, "prev"):
                    wait_apart(sp, base_stored, 16 * b)
                    sp.dma_start(xres[:, :, :], rows(x_flat, b - 1)).then_inc(xres_loaded, 16)
                if here(b, "cur"):
                    place_stack(b, 3)
                    place_max(b, 1)
                    for dst, w in ((wgs, wg), (wps, wp)):
                        sp.dma_start(dst[:, bass.ds(b, 1), :],
                                     w.rearrange("n (k p) f -> p (n k) f", p=P)[:, bass.ds(b, 1), :]).then_inc(up_loaded, 16)
                if here(b, "next"):
                    place_stack(b + 1, 0, which=(0,))
                if here(b, "cur"):
                    place_max(b, 2)
                if here(b, "next"):
                    place_stack(b + 1, 0, which=(1,))

            place_stack(0, 0)
            sp.wait_ge(iota_set, IOTAS)
            for i in range(BEYOND):
                row = NE * REGION + i * P
                sp.dma_start(slots_d[row:row + P, :], padrow[:, :]).then_inc(beyond_placed, 16)
            sp.dma_start(out[B * N:B * N + P, :], padrow[:, 0:E]).then_inc(base_stored, 16)
            over_batches(sp, body)
            sp.wait_ge(s2_full, B * UNITS)
            sp.dma_start(wos, wo.rearrange("n (f p) e -> p (n f) e", p=P)).then_inc(down_loaded, 16)
            sp.wait_ge(pads_set, 1)
            for e in range(NE):
                slot = sp.value_load(padu[0:1, e:e + 1], min_val=0, max_val=NE * REGION - P)
                sp.dma_start(slots_d[bass.ds(slot, P), :], padrow[:, :]).then_inc(pad_placed, 16)
            for c in range(TOP):
                sp.wait_ge(srow_placed[c], 16 * TT * B)
            sp.wait_ge(pad_placed, 16 * NE)
            sp.wait_ge(beyond_placed, 16 * BEYOND)
            sp.wait_ge(table_set, 1)

            def load_tile(i):
                if is_reg(i) or i > 0:
                    wait_apart(sp, tinT_full, i)
                    wait_apart(sp, meta_taken, i)
                slot = sp.value_load(tabu[0:1, 0, bass.ds(i, 1)], min_val=0, max_val=slots_d.shape[0] - P)
                sp.dma_start(tin[:, :], slots_d[bass.ds(slot, P), :]).then_inc(tin_loaded, 16)

            load_tile(0)
            with sp.Fori(1, NT) as i:
                load_tile(i)
            sp.wait_ge(base_stored, 16 * (B + 1))
            sp.wait_ge(y_added, 16 * NT)


_INS = ["x", "Wq", "bq", "Wk", "bk", "Wv", "bv", "Wo"]
_FFN = ["router_w", "router_b", "temperature", "wg", "wp", "wo"]


def kernel(**inputs):
    import numpy as _np
    import concourse.bacc as _bacc
    from concourse import mybir as _mybir
    from concourse.bass_utils import run_bass_kernel_spmd as _run

    nc = _bacc.Bacc("TRN2", target_bir_lowering=False, num_devices=1)
    arrays, args = {}, []
    for name in ["L0_attn_" + n for n in _INS] + ["L0_ffn_" + n for n in _FFN]:
        a = _np.ascontiguousarray(inputs[name])
        arrays[f"in_{name}"] = a
        args.append(nc.dram_tensor(f"in_{name}", a.shape, _mybir.dt.from_np(a.dtype), kind="ExternalInput").ap())
    shape = inputs["L0_attn_x"].shape
    tokens = shape[0] * shape[1]
    args.append(nc.dram_tensor("out_0", (tokens + P, shape[2]), _mybir.dt.float32, kind="ExternalOutput").ap())
    build(nc, *args)
    r = _run(nc, [arrays], core_ids=[0])
    return r.results[0]["out_0"][:tokens].reshape(shape)
```
